# Optimizing a Trainium2 kernel written in Bass

```python
import numpy as np
import jax
import jax.numpy as jnp

def _softmax(x, axis=-1):
    return jax.nn.softmax(x, axis=axis)

def _gelu(x):
    return jax.nn.gelu(x, approximate=True)

def _silu(x):
    return jax.nn.silu(x)

def _sigmoid(x):
    return jax.nn.sigmoid(x)

def _layernorm(x, axis=-1, eps=1e-05):
    m = jnp.mean(x, axis=axis, keepdims=True)
    v = jnp.var(x, axis=axis, keepdims=True)
    return (x - m) / jnp.sqrt(v + eps)

def _scatter_add(tgt, idx, src, axis=0):
    return tgt.at[idx].add(src)

def _segment_sum(src, seg, n):
    return jax.ops.segment_sum(src, seg, n)
kernel_name = 'mk_adj_resnorm_d1_adj_r2_7becdf'

def setup_inputs(seed: int=0):
    np.random.seed(seed)
    _w = jnp.asarray

    def _rec_inputs():
        import jax
        import jax.numpy as jnp
        _gk = jax.random.key(seed)
        x = -0.0002928 + 1 * jax.random.normal(jax.random.fold_in(_gk, 1), (64, 128, 256), jnp.float32)
        _a = jax.random.bernoulli(jax.random.fold_in(_gk, 2), 0.125, (64, 128, 128))
        _a = jnp.logical_or(_a, jnp.swapaxes(_a, -1, -2))
        _a = jnp.logical_or(_a, jnp.eye(128, dtype=bool))
        adj = _a.astype(jnp.int32)
        return (x, adj)
    x, adj = _rec_inputs()

    def _L0_gnn_setup():
        import jax, jax.numpy as jnp
        import numpy as np
        L = 3
        D = 256
        B, N = (8, 512)
        EPS = 1e-05

        def layernorm(x, gamma, beta):
            mu = jnp.mean(x, axis=-1, keepdims=True)
            var = jnp.var(x, axis=-1, keepdims=True)
            return (x - mu) * jax.lax.rsqrt(var + EPS) * gamma + beta
        key = jax.random.key(seed)
        ks = jax.random.split(key, 12)
        s = 1.0 / np.sqrt(D)
        node_features = jax.random.normal(ks[0], (B, N, D), dtype=jnp.float32)
        adjacency_matrix = jax.random.randint(ks[1], (B, N, N), 0, 2, dtype=jnp.int32)
        return {'node_features': node_features, 'adjacency_matrix': adjacency_matrix, 'attn_w': jax.random.normal(ks[2], (L, 2 * D), dtype=jnp.float32) * (1.0 / np.sqrt(2 * D)), 'attn_b': jax.random.normal(ks[3], (L,), dtype=jnp.float32) * 0.01, 'W1': jax.random.normal(ks[4], (L, D, 4 * D), dtype=jnp.float32) * s, 'b1': jnp.zeros((L, 4 * D), dtype=jnp.float32), 'W2': jax.random.normal(ks[5], (L, 4 * D, D), dtype=jnp.float32) * (1.0 / np.sqrt(4 * D)), 'b2': jnp.zeros((L, D), dtype=jnp.float32), 'g1': jnp.ones((L, D), dtype=jnp.float32), 'beta1': jnp.zeros((L, D), dtype=jnp.float32), 'g2': jnp.ones((L, D), dtype=jnp.float32), 'beta2': jnp.zeros((L, D), dtype=jnp.float32)}
    _L0_gnn_all = _L0_gnn_setup()
    _L0_gnn_in = {k: v for k, v in _L0_gnn_all.items() if k in ('attn_w', 'attn_b', 'W1', 'b1', 'W2', 'b2', 'g1', 'beta1', 'g2', 'beta2')}
    del _L0_gnn_all
    return {'x': x, 'adj': adj, 'L0_gnn_attn_w': _L0_gnn_in['attn_w'], 'L0_gnn_attn_b': _L0_gnn_in['attn_b'], 'L0_gnn_W1': _L0_gnn_in['W1'], 'L0_gnn_b1': _L0_gnn_in['b1'], 'L0_gnn_W2': _L0_gnn_in['W2'], 'L0_gnn_b2': _L0_gnn_in['b2'], 'L0_gnn_g1': _L0_gnn_in['g1'], 'L0_gnn_beta1': _L0_gnn_in['beta1'], 'L0_gnn_g2': _L0_gnn_in['g2'], 'L0_gnn_beta2': _L0_gnn_in['beta2']}

def reference(x, adj, L0_gnn_attn_w, L0_gnn_attn_b, L0_gnn_W1, L0_gnn_b1, L0_gnn_W2, L0_gnn_b2, L0_gnn_g1, L0_gnn_beta1, L0_gnn_g2, L0_gnn_beta2):
    import jax
    import jax.numpy as jnp

    def _L0_gnn_ref(node_features, adjacency_matrix, attn_w, attn_b, W1, b1, W2, b2, g1, beta1, g2, beta2):
        import jax, jax.numpy as jnp
        import numpy as np
        L = 3
        D = 256
        B, N = (8, 512)
        EPS = 1e-05

        def layernorm(x, gamma, beta):
            mu = jnp.mean(x, axis=-1, keepdims=True)
            var = jnp.var(x, axis=-1, keepdims=True)
            return (x - mu) * jax.lax.rsqrt(var + EPS) * gamma + beta
        n = adjacency_matrix.shape[-1]
        mask = adjacency_matrix.astype(jnp.float32) + jnp.eye(n, dtype=jnp.float32) > 0
        x = node_features
        d = x.shape[-1]
        for l in range(attn_w.shape[0]):
            si = x @ attn_w[l, :d]
            sj = x @ attn_w[l, d:]
            scores = si[:, :, None] + sj[:, None, :] + attn_b[l]
            scores = jnp.where(scores >= 0, scores, 0.2 * scores)
            scores = jnp.where(mask, scores, -jnp.inf)
            attn = jax.nn.softmax(scores, axis=-1)
            agg = jnp.einsum('bij,bjd->bid', attn, x)
            h = layernorm(x + agg, g1[l], beta1[l])
            ff = jax.nn.gelu(h @ W1[l] + b1[l], approximate=False) @ W2[l] + b2[l]
            x = layernorm(h + ff, g2[l], beta2[l])
        return x
    x = _layernorm(x + _L0_gnn_ref(x, adj, L0_gnn_attn_w, L0_gnn_attn_b, L0_gnn_W1, L0_gnn_b1, L0_gnn_W2, L0_gnn_b2, L0_gnn_g1, L0_gnn_beta1, L0_gnn_g2, L0_gnn_beta2), axis=-1)
    return x

_drawn_inputs = setup_inputs


def setup_inputs(seed=0):
    import zlib

    import numpy as np

    out = dict(_drawn_inputs(seed))
    spreads = {'L0_gnn_b1': (0.0, 0.1),
     'L0_gnn_b2': (0.0, 0.1),
     'L0_gnn_g1': (1.0, 0.2),
     'L0_gnn_beta1': (0.0, 0.1),
     'L0_gnn_g2': (1.0, 0.2),
     'L0_gnn_beta2': (0.0, 0.1)}
    factors = {'L0_gnn_attn_b': 64.0}
    for name, (base, spread) in spreads.items():
        noise = np.random.default_rng([zlib.crc32(name.encode()), seed]).standard_normal(out[name].shape)
        drawn = base * np.exp(spread * noise) if base else spread * noise
        out[name] = jnp.asarray(drawn.astype(out[name].dtype))
    for name, factor in factors.items():
        out[name] = (out[name] * factor).astype(out[name].dtype)
    return out
```

```python
from contextlib import ExitStack

import concourse.bass as bass
from concourse import mybir

ALU = mybir.AluOpType
ACT = mybir.ActivationFunctionType
F32 = mybir.dt.float32
F32R = mybir.dt.float32r
I32 = mybir.dt.int32
AX_X = mybir.AxisListType.X

P = 128
EPS = 1e-5
MASKED = 1e30
SLOPE = 0.2


def gnn_layers_resnorm_kernel(nc, x, adj, attn_w, attn_b, W1, b1, W2, b2, g1, beta1, g2, beta2, out):
    B, N, D = x.shape
    L, _, F = W1.shape
    G = 4
    NG = B // G
    U = L * NG
    KD = D // P
    KF = F // P
    T = G * N
    GD = G * D
    assert N == P and T == 512 and NG == 16 and KD == 2 and KF == 8

    with ExitStack() as ctx:
        def sb(name, shape, dt=F32):
            return ctx.enter_context(nc.sbuf_tensor(name, shape, dt))

        def psum(name, shape):
            return ctx.enter_context(nc.psum_tensor(name, shape, F32))

        def sem(name):
            return ctx.enter_context(nc.semaphore(name))

        X = sb("X", [P, B * D])
        w1_raw = sb("w1_raw", [P, KD, F])
        w2_raw = sb("w2_raw", [P, KF, D])
        w1_hi = sb("w1_hi", [P, KD, F], F32R)
        w1_lo = sb("w1_lo", [P, KD, F], F32R)
        w2_hi = sb("w2_hi", [P, KF, D], F32R)
        w2_lo = sb("w2_lo", [P, KF, D], F32R)
        wi_rows = sb("wi_rows", [P, L, D])
        wj_rows = sb("wj_rows", [P, L, D])
        bias_attn = sb("bias_attn", [P, L])
        g1_rows = sb("g1_rows", [P, L, D])
        c1_rows = sb("c1_rows", [P, L, D])
        g2_rows = sb("g2_rows", [P, L, D])
        beta2_rows = sb("beta2_rows", [P, L, D])
        g1_cols = sb("g1_cols", [P, L, KD])
        beta1_cols = sb("beta1_cols", [P, L, KD])
        b1_cols = sb("b1_cols", [P, L, KF])
        ident = sb("ident", [P, P])
        neg_ident = sb("neg_ident", [P, P])
        neg_ident_r = sb("neg_ident_r", [P, P], F32R)
        minus_half = sb("minus_half", [P, G])
        adj_in = sb("adj_in", [P, T], I32)
        offset = sb("offset", [P, T])
        dot_junk = sb("dot_junk", [P, 2, D])
        si_raw = sb("si_raw", [P, G])
        neg_si = sb("neg_si", [P, G])
        sj = sb("sj", [P, G])
        sj_hi = sb("sj_hi", [P, G], F32R)
        sj_lo = sb("sj_lo", [P, G], F32R)
        neg_scores = sb("neg_scores", [P, T])
        neg_max = sb("neg_max", [P, G])
        prob = sb("prob", [P, T])
        row_sum = sb("row_sum", [P, G])
        row_inv = sb("row_inv", [P, G])
        pt_hi = sb("pt_hi", [P, T], F32R)
        pt_lo = sb("pt_lo", [P, T], F32R)
        x_hi = sb("x_hi", [P, GD], F32R)
        x_lo = sb("x_lo", [P, GD], F32R)
        res1 = sb("res1", [P, GD])
        stats1 = sb("stats1", [P, G, 6])
        moments1 = sb("moments1", [P, G, 2])
        scratch1 = sb("scratch1", [P, 4, G])
        z1 = sb("z1", [P, GD])
        q = sb("q", [P, GD])
        ht = sb("ht", [P, KD, T])
        ht_hi = sb("ht_hi", [P, KD, T], F32R)
        ht_lo = sb("ht_lo", [P, KD, T], F32R)
        act_out = sb("act_out", [P, 2, T])
        act_hi = sb("act_hi", [P, KF, T], F32R)
        act_lo = sb("act_lo", [P, KF, T], F32R)
        res2 = sb("res2", [P, GD])
        stats2 = sb("stats2", [P, G, 6])
        moments2 = sb("moments2", [P, G, 2])
        scratch2 = sb("scratch2", [P, 4, G])
        y = sb("y", [P, GD])
        stats3 = sb("stats3", [P, G, 6])
        moments3 = sb("moments3", [P, G, 2])
        scratch3 = sb("scratch3", [P, 4, G])

        ps_mix = psum("ps_mix", [P, 2, T])
        ps_mlp = psum("ps_mlp", [P, 2, T])
        ps_hid = [psum("ps_hid0", [P, T]), psum("ps_hid1", [P, T])]
        ps_scores = psum("ps_scores", [P, T])
        ps_pt = psum("ps_pt", [P, T])

        params_in = sem("params_in")
        x_in = sem("x_in")
        adj_landed = sem("adj_landed")
        w1_in = sem("w1_in")
        w2_in = sem("w2_in")
        x_first_in = sem("x_first_in")
        stored = sem("stored")
        norm_const = sem("norm_const")
        neg_ident_done = sem("neg_ident_done")
        ident_done = sem("ident_done")
        w1_split = sem("w1_split")
        w1_hi_done = sem("w1_hi_done")
        w2_split = sem("w2_split")
        w2_hi_done = sem("w2_hi_done")
        c1_done = sem("c1_done")
        dots_done = sem("dots_done")
        sj_hi_done = sem("sj_hi_done")
        sj_done = sem("sj_done")
        neg_si_done = sem("neg_si_done")
        blocked_done = sem("blocked_done")
        offset_done = sem("offset_done")
        scores_mm = sem("scores_mm")
        neg_scores_done = sem("neg_scores_done")
        leaky_done = sem("leaky_done")
        neg_max_done = sem("neg_max_done")
        prob_done = sem("prob_done")
        row_inv_done = sem("row_inv_done")
        pt_mm = sem("pt_mm")
        pt_hi_done = sem("pt_hi_done")
        pt_done = sem("pt_done")
        x_hi_done = sem("x_hi_done")
        x_lo_done = sem("x_lo_done")
        mix_mm = sem("mix_mm")
        res1_done = sem("res1_done")
        stats1_done = sem("stats1_done")
        moments1_done = sem("moments1_done")
        norm1_step = sem("norm1_step")
        z1_done = sem("z1_done")
        q_step = sem("q_step")
        zt_mm = sem("zt_mm")
        ht_done = sem("ht_done")
        ht_hi_done = sem("ht_hi_done")
        ht_lo_done = sem("ht_lo_done")
        hid_mm = sem("hid_mm")
        gelu_done = sem("gelu_done")
        act_hi_done = sem("act_hi_done")
        act_lo_done = sem("act_lo_done")
        mlp_mm = sem("mlp_mm")
        res2_done = sem("res2_done")
        stats2_done = sem("stats2_done")
        moments2_done = sem("moments2_done")
        norm2_step = sem("norm2_step")
        z2_done = sem("z2_done")
        x_scaled = sem("x_scaled")
        x_done = sem("x_done")
        res3_done = sem("res3_done")
        stats3_done = sem("stats3_done")
        moments3_done = sem("moments3_done")
        norm3_step = sem("norm3_step")
        y_done = sem("y_done")
        held = sem("held")

        LAST = (L - 1) * NG
        N_PARAMS = 8 + 2 * KD + L

        def group(u):
            return u % NG

        def layer(u):
            return u // NG

        def xg(u):
            return X[:, bass.ds(group(u) * GD, GD)]

        def xb(u, b):
            return X[:, bass.ds(group(u) * GD + b * D, D)]

        def row(params, u):
            return params[:, bass.ds(layer(u), 1), :].rearrange("p o d -> p (o d)")

        def rows4(params, u):
            return params[:, bass.ds(layer(u), 1), :].broadcast_to([P, G, D])

        def col(params, u, c):
            return params[:, bass.ds(layer(u), 1), c]

        def by_graph(ap):
            return ap.rearrange("p (b d) -> p b d", b=G)

        def need(eng, semaphore, value):
            if not isinstance(value, int) or value > 0:
                eng.wait_ge(semaphore, value)

        def hold(eng, semaphore, value):
            need(eng, semaphore, value)
            if not isinstance(value, int):
                eng.sem_inc(held, 1)

        def run_steps(eng, start, step, swap_weights=None, enter_layer=None):
            start()
            step(0, close=None)
            with eng.Fori(0, L - 1) as l:
                if enter_layer is not None:
                    enter_layer(l + 1)
                with eng.Fori(1, NG) as g:
                    step(l * NG + g, close="x")
                if swap_weights is not None:
                    swap_weights(l + 1)
                step(l * NG + NG, close="x")
            with eng.Fori(LAST + 1, U - 3) as t:
                step(t, close="y")
            step(U - 3, close="y", dots=False)
            step(U - 2, close="y", dots=False, scores=False)
            step(U - 1, close="y", dots=False, scores=False, mix=False)
            step(U, close="y", dots=False, scores=False, mix=False, mlp=False)

        ctx.enter_context(nc.allow_non_contiguous_dma(reason="3072 small parameters go down the partitions, once"))
        block = ctx.enter_context(nc.Block())

        @block.sync
        def _(sp):
            def param(dst, src):
                sp.dma_start(dst, src).then_inc(params_in, 16)

            def rows_of(src):
                return src.rearrange("(o l) d -> o l d", o=1).broadcast_to([P, L, src.shape[1]])

            def load_x(g):
                sp.dma_start(by_graph(X[:, bass.ds(g * GD, GD)]),
                             x[bass.ds(g * G, G), :, :].rearrange("b i d -> i b d")).then_inc(x_in, 16)

            def load_adj(u):
                need(sp, blocked_done, u)
                sp.dma_start(by_graph(adj_in[:, :]),
                             adj[bass.ds(group(u) * G, G), :, :].rearrange("b i j -> i b j")
                             ).then_inc(adj_landed, 16)
                hold(sp, adj_landed, 16 * u + 16)

            def load_weights(l):
                need(sp, w1_split, l)
                sp.dma_start(w1_raw[:, :, :], W1[bass.ds(l, 1), :, :].rearrange("o (k p) f -> p (o k) f", p=P)
                             ).then_inc(w1_in, 16)
                need(sp, w2_split, l)
                sp.dma_start(w2_raw[:, :, :], W2[bass.ds(l, 1), :, :].rearrange("o (k p) d -> p (o k) d", p=P)
                             ).then_inc(w2_in, 16)

            def start():
                load_x(0)
                param(wi_rows[:, :, :], rows_of(attn_w[:, 0:D]))
                param(wj_rows[:, :, :], rows_of(attn_w[:, D:2 * D]))
                param(bias_attn[:, :], attn_b.rearrange("(o l) -> o l", o=1).broadcast_to([P, L]))
                load_adj(0)
                for k in range(KD):
                    param(g1_cols[:, :, k], g1[:, k * P:(k + 1) * P].rearrange("l p -> p l"))
                    param(beta1_cols[:, :, k], beta1[:, k * P:(k + 1) * P].rearrange("l p -> p l"))
                param(g1_rows[:, :, :], rows_of(g1))
                param(c1_rows[:, :, :], rows_of(beta1))
                param(y[:, 0:L * D].rearrange("p (l d) -> p l d", l=L), rows_of(b2))
                param(g2_rows[:, :, :], rows_of(g2))
                param(beta2_rows[:, :, :], rows_of(beta2))
                for l in range(L):
                    param(b1_cols[:, l, :], b1[l, :].rearrange("(k p) -> p k", p=P))
                load_weights(0)
                sp.wait_ge(x_in, 16)
                load_x(1)
                load_adj(1)
                sp.wait_ge(x_in, 32)
                with sp.Fori(2, NG) as g:
                    load_x(g)
                    hold(sp, x_in, 16 * g + 16)

            def step(t, close, dots=True, scores=True, mix=True, mlp=True):
                if close == "y":
                    n = t - 1 - LAST
                    need(sp, stored, 16 * n)
                    sp.dma_start(by_graph(y[:, :]),
                                 x[bass.ds(group(t - 1) * G, G), :, :].rearrange("b i d -> i b d")
                                 ).then_inc(x_first_in, 16)
                if scores:
                    load_adj(t + 2)
                if close == "y":
                    sp.wait_ge(y_done, G * n + G)
                    sp.dma_start(out[bass.ds(group(t - 1) * G, G), :, :].rearrange("b i d -> i b d"),
                                 by_graph(y[:, :])).then_inc(stored, 16)

            run_steps(sp, start, step, enter_layer=load_weights)
            sp.wait_ge(stored, 16 * NG)

        @block.gpsimd
        def _(pool):
            def offsets(u):
                pool.wait_ge(blocked_done, u + 1)
                hold(pool, neg_si_done, u + 1)
                for b in range(G):
                    pool.tensor_scalar(offset[:, b * N:(b + 1) * N], offset[:, b * N:(b + 1) * N], MASKED,
                                       neg_si[:, b:b + 1], ALU.mult, ALU.add).then_inc(offset_done, 1)

            def normalise(n, first, moments_done, moments, scratch, norm_step, src, dst, dst_done):
                var, rstd, nmean, shift = (scratch[:, i, :] for i in range(4))
                pool.wait_ge(moments_done, G * n + G + first)
                hold(pool, dst_done, G * n + first)
                pool.tensor_scalar(var, moments[:, :, 1], EPS, None, ALU.add).then_inc(norm_step, 1)
                pool.tensor_scalar(nmean, moments[:, :, 0], -1.0, None, ALU.mult).then_inc(norm_step, 1)
                pool.wait_ge(norm_step, 4 * n + 2 + first)
                pool.tensor_tensor(rstd, var, minus_half[:, :], ALU.pow).then_inc(norm_step, 1)
                pool.wait_ge(norm_step, 4 * n + 3 + first)
                pool.tensor_tensor(shift, nmean, rstd, ALU.mult).then_inc(norm_step, 1)
                hold(pool, norm_step, 4 * n + 4 + first)
                for b in range(G):
                    pool.tensor_scalar(dst[:, b * D:(b + 1) * D], src[:, b * D:(b + 1) * D], rstd[:, b:b + 1],
                                       shift[:, b:b + 1], ALU.mult, ALU.add).then_inc(dst_done, 1)

            def normalise1(u):
                need(pool, zt_mm, KD * u)
                need(pool, q_step, 2 * u)
                normalise(u, 0, moments1_done, moments1, scratch1, norm1_step, res1, z1, z1_done)

            def residual1(u):
                pool.wait_ge(z1_done, G * u + G)
                pool.wait_ge(c1_done, 1)
                hold(pool, res2_done, 2 * u)
                pool.tensor_tensor(by_graph(q[:, :]), by_graph(z1[:, :]), rows4(g1_rows, u), ALU.mult
                                   ).then_inc(q_step, 1)
                hold(pool, q_step, 2 * u + 1)
                pool.tensor_tensor(by_graph(q[:, :]), by_graph(q[:, :]), rows4(c1_rows, u), ALU.add
                                   ).then_inc(q_step, 1)

            def normalise2(u):
                pool.wait_ge(x_done, u + 1)
                normalise(u, 1, moments2_done, moments2, scratch2, norm2_step, res2, res2, z2_done)

            def update_x(u):
                hold(pool, z2_done, G * u + G + 1)
                pool.tensor_tensor(by_graph(xg(u)), by_graph(res2[:, :]), rows4(g2_rows, u), ALU.mult
                                   ).then_inc(x_scaled, 1)
                hold(pool, x_scaled, u + 2)
                pool.tensor_tensor(by_graph(xg(u)), by_graph(xg(u)), rows4(beta2_rows, u), ALU.add
                                   ).then_inc(x_done, 1)

            def start():
                for tile in (ident, neg_ident):
                    pool.memset(tile[:, :], 0.0).then_inc(ident_done, 1)
                pool.memset(minus_half[:, :], -0.5).then_inc(norm_const, 1)
                for i, free in enumerate((z2_done, x_scaled, x_done)):
                    pool.memset(res2[:, i:i + 1], 0.0).then_inc(free, 1)
                pool.memset(scratch2[:, 0, 0:1], 0.0).then_inc(norm2_step, 1)
                pool.wait_ge(ident_done, 2)
                for tile, fill in ((ident, 1.0), (neg_ident, -1.0)):
                    pool.affine_select(out=tile[:, :], in_=tile[:, :], compare_op=ALU.not_equal, fill=fill, base=0,
                                       pattern=[[-1, P]], channel_multiplier=1).then_inc(ident_done, 1)
                pool.wait_ge(params_in, 16 * N_PARAMS)
                pool.tensor_tensor(c1_rows[:, :, :], c1_rows[:, :, :], y[:, 0:L * D].rearrange("p (l d) -> p l d", l=L), ALU.add
                                   ).then_inc(c1_done, 1)
                pool.wait_ge(norm_const, 1)
                offsets(0)
                normalise1(0)
                offsets(1)

            def step(t, close, dots=True, scores=True, mix=True, mlp=True):
                if mlp:
                    residual1(t)
                if close:
                    normalise2(t - 1)
                if mix:
                    normalise1(t + 1)
                if scores:
                    offsets(t + 2)
                if close:
                    update_x(t - 1)
                if close == "y":
                    n = t - 1 - LAST
                    normalise(n, 0, moments3_done, moments3, scratch3, norm3_step, y, y, y_done)

            run_steps(pool, start, step)

        @block.scalar
        def _(act):
            def split_weights(l):
                act.wait_ge(w1_in, 16 * l + 16)
                need(act, hid_mm, l * (NG * KF))
                act.activation(w1_hi[:, :, :], w1_raw[:, :, :], ACT.Copy).then_inc(w1_hi_done, 1)
                act.wait_ge(w2_in, 16 * l + 16)
                need(act, mlp_mm, l * (NG * 2))
                act.activation(w2_hi[:, :, :], w2_raw[:, :, :], ACT.Copy).then_inc(w2_hi_done, 1)

            def x_high(u):
                need(act, mix_mm, 2 * u)
                need(act, x_lo_done, u)
                act.activation(x_hi[:, :], xg(u), ACT.Copy).then_inc(x_hi_done, 1)

            def softmax_numerators(u):
                act.wait_ge(neg_max_done, u + 1)
                need(act, pt_mm, u)
                need(act, row_inv_done, u)
                for b in range(G):
                    act.activation(prob[:, b * N:(b + 1) * N], neg_scores[:, b * N:(b + 1) * N], ACT.Exp,
                                   bias=neg_max[:, b:b + 1], scale=-1.0, accum_out=row_sum[:, b:b + 1]
                                   ).then_inc(prob_done, 1)

            def pt_high(u):
                act.wait_ge(pt_mm, u + 1)
                need(act, mix_mm, 2 * u)
                need(act, pt_done, u)
                act.activation(pt_hi[:, :], ps_pt[:, :], ACT.Copy).then_inc(pt_hi_done, 1)

            def h_transposed(u):
                for k in range(KD):
                    act.wait_ge(zt_mm, KD * u + k + 1)
                    if k == 0:
                        need(act, ht_lo_done, u)
                        need(act, hid_mm, KF * u)
                    for dst, done in ((ht, ht_done), (ht_hi, ht_hi_done)):
                        act.activation(dst[:, k, :], ps_mix[:, k, :], ACT.Identity, bias=col(beta1_cols, u, k),
                                       scale=col(g1_cols, u, k)).then_inc(done, 1)

            def gelu(u, c):
                act.wait_ge(hid_mm, KF * u + c + 1)
                need(act, act_lo_done, KF * u + c - 1)
                act.activation(act_out[:, c % 2, :], ps_hid[c % 2][:, :], ACT.Gelu, bias=col(b1_cols, u, c)
                               ).then_inc(gelu_done, 1)
                act.wait_ge(gelu_done, KF * u + c + 1)
                if c == 0:
                    need(act, mlp_mm, 2 * u)
                act.activation(act_hi[:, c, :], act_out[:, c % 2, :], ACT.Copy).then_inc(act_hi_done, 1)

            def start():
                act.wait_ge(x_in, 16)
                x_high(0)
                act.wait_ge(params_in, 16 * N_PARAMS)
                softmax_numerators(0)
                pt_high(0)
                split_weights(0)
                h_transposed(0)
                act.wait_ge(x_in, 32)
                x_high(1)
                softmax_numerators(1)
                pt_high(1)

            def step(t, close, dots=True, scores=True, mix=True, mlp=True):
                if mlp:
                    for c in range(KF):
                        gelu(t, c)
                if scores:
                    x_high(t + 2)
                    softmax_numerators(t + 2)
                if mix:
                    h_transposed(t + 1)
                if scores:
                    pt_high(t + 2)

            run_steps(act, start, step, swap_weights=split_weights)

        @block.vector
        def _(dve):
            def split_weights(l):
                dve.wait_ge(w1_hi_done, l + 1)
                need(dve, hid_mm, l * (NG * KF))
                dve.tensor_tensor(w1_lo[:, :, :], w1_raw[:, :, :], w1_hi[:, :, :].bitcast(F32), ALU.subtract
                                  ).then_inc(w1_split, 1)
                dve.wait_ge(w2_hi_done, l + 1)
                need(dve, mlp_mm, l * (NG * 2))
                dve.tensor_tensor(w2_lo[:, :, :], w2_raw[:, :, :], w2_hi[:, :, :].bitcast(F32), ALU.subtract
                                  ).then_inc(w2_split, 1)

            def token_dots(u):
                dve.wait_ge(x_in, 16 * group(u) + 16)
                need(dve, neg_si_done, u)
                need(dve, sj_done, u)
                for n in range(2 * G):
                    b = n % G
                    sign, weights, dot = (-1.0, wi_rows, si_raw) if n < G else (1.0, wj_rows, sj)
                    need(dve, dots_done, 2 * G * u + n - 1)
                    dve.scalar_tensor_tensor(dot_junk[:, n % 2, :], xb(u, b), sign, row(weights, u), ALU.mult,
                                             ALU.mult, accum_out=dot[:, b:b + 1]).then_inc(dots_done, 1)
                dve.wait_ge(dots_done, 2 * G * u + G)
                need(dve, offset_done, G * u)
                dve.tensor_scalar(neg_si[:, :], si_raw[:, :], bias_attn[:, bass.ds(layer(u), 1)], None, ALU.subtract
                                  ).then_inc(neg_si_done, 1)
                dve.wait_ge(dots_done, 2 * G * u + 2 * G)
                need(dve, scores_mm, u)
                dve.tensor_copy(sj_hi[:, :], sj[:, :]).then_inc(sj_hi_done, 1)
                dve.wait_ge(sj_hi_done, u + 1)
                dve.tensor_tensor(sj_lo[:, :], sj[:, :], sj_hi[:, :].bitcast(F32), ALU.subtract).then_inc(sj_done, 1)

            def compare(u):
                dve.wait_ge(adj_landed, 16 * u + 16)
                need(dve, neg_scores_done, u)
                dve.tensor_tensor(by_graph(offset[:, :]), by_graph(adj_in[:, :]),
                                  neg_ident[:, :].unsqueeze(1).broadcast_to([P, G, N]), ALU.is_le
                                  ).then_inc(blocked_done, 1)

            def masked_scores(u):
                dve.wait_ge(scores_mm, u + 1)
                dve.wait_ge(offset_done, G * u + G)
                need(dve, prob_done, G * u)
                dve.tensor_tensor(neg_scores[:, :], ps_scores[:, :], offset[:, :], ALU.add).then_inc(neg_scores_done, 1)
                dve.wait_ge(neg_scores_done, u + 1)
                dve.scalar_tensor_tensor(neg_scores[:, :], neg_scores[:, :], SLOPE, neg_scores[:, :], ALU.mult, ALU.min
                                         ).then_inc(leaky_done, 1)
                dve.wait_ge(leaky_done, u + 1)
                dve.tensor_reduce(neg_max[:, :], by_graph(neg_scores[:, :]), AX_X, ALU.min).then_inc(neg_max_done, 1)

            def invert_sums(u):
                dve.wait_ge(prob_done, G * u + G)
                need(dve, res1_done, G * u)
                dve.reciprocal(row_inv[:, :], row_sum[:, :]).then_inc(row_inv_done, 1)

            def x_low(u):
                dve.wait_ge(x_hi_done, u + 1)
                need(dve, mix_mm, 2 * u)
                dve.tensor_tensor(x_lo[:, :], xg(u), x_hi[:, :].bitcast(F32), ALU.subtract).then_inc(x_lo_done, 1)

            def pt_low(u):
                dve.wait_ge(pt_hi_done, u + 1)
                need(dve, mix_mm, 2 * u)
                dve.tensor_tensor(pt_lo[:, :], ps_pt[:, :], pt_hi[:, :].bitcast(F32), ALU.subtract).then_inc(pt_done, 1)

            def add_mix(u):
                dve.wait_ge(row_inv_done, u + 1)
                need(dve, z1_done, G * u)
                for b in range(G):
                    if b % 2 == 0:
                        dve.wait_ge(mix_mm, 2 * u + b // 2 + 1)
                    dve.scalar_tensor_tensor(res1[:, b * D:(b + 1) * D], ps_mix[:, b // 2, (b % 2) * D:(b % 2 + 1) * D],
                                             row_inv[:, b:b + 1], xb(u, b), ALU.mult, ALU.add).then_inc(res1_done, 1)

            def statistics(n, first, src, src_done, per_src, stats, stats_done, moments, moments_done, norm_step):
                need(dve, moments_done, G * n + first)
                for b in range(G):
                    if b % (G // per_src) == 0:
                        dve.wait_ge(src_done, per_src * n + b // (G // per_src) + 1)
                    dve.bn_stats(stats[:, b, :], src[:, b * D:(b + 1) * D]).then_inc(stats_done, 1)
                need(dve, norm_step, 4 * n + first)
                hold(dve, stats_done, G * n + G)
                for b in range(G):
                    dve.bn_aggr(moments[:, b, :], stats[:, b, :]).then_inc(moments_done, 1)

            def statistics1(u):
                statistics(u, 0, res1, res1_done, G, stats1, stats1_done, moments1, moments1_done, norm1_step)

            def h_low(u):
                dve.wait_ge(ht_hi_done, KD * u + KD)
                dve.wait_ge(ht_done, KD * u + KD)
                need(dve, hid_mm, KF * u)
                dve.tensor_tensor(ht_lo[:, :, :], ht[:, :, :], ht_hi[:, :, :].bitcast(F32), ALU.subtract
                                  ).then_inc(ht_lo_done, 1)

            def act_low(u, c):
                dve.wait_ge(act_hi_done, KF * u + c + 1)
                if c == 0:
                    need(dve, mlp_mm, 2 * u)
                dve.tensor_tensor(act_lo[:, c, :], act_out[:, c % 2, :], act_hi[:, c, :].bitcast(F32), ALU.subtract
                                  ).then_inc(act_lo_done, 1)

            def add_mlp(u):
                dve.wait_ge(q_step, 2 * u + 2)
                dve.wait_ge(z2_done, G * u + 1)
                dve.wait_ge(x_scaled, u + 1)
                for i in range(2):
                    dve.wait_ge(mlp_mm, 2 * u + i + 1)
                    dve.tensor_tensor(res2[:, i * T:(i + 1) * T], ps_mlp[:, i, :], q[:, i * T:(i + 1) * T], ALU.add
                                      ).then_inc(res2_done, 1)

            def add_input(u):
                n = u - LAST
                dve.wait_ge(x_done, u + 2)
                dve.wait_ge(x_first_in, 16 * n + 16)
                dve.tensor_tensor(y[:, :], xg(u), y[:, :], ALU.add).then_inc(res3_done, 1)
                statistics(n, 0, y, res3_done, 1, stats3, stats3_done, moments3, moments3_done, norm3_step)

            def scores_to_mix(u):
                masked_scores(u)
                x_low(u)
                invert_sums(u)
                pt_low(u)

            def start():
                dve.memset(moments2[:, :, :], 0.0).then_inc(moments2_done, 1)
                dve.wait_ge(ident_done, 4)
                dve.tensor_copy(neg_ident_r[:, :], neg_ident[:, :]).then_inc(neg_ident_done, 1)
                dve.wait_ge(params_in, 16 * N_PARAMS)
                token_dots(0)
                compare(0)
                scores_to_mix(0)
                split_weights(0)
                add_mix(0)
                statistics1(0)
                h_low(0)
                token_dots(1)
                compare(1)
                scores_to_mix(1)
                token_dots(2)

            def step(t, close, dots=True, scores=True, mix=True, mlp=True):
                def low(c):
                    if mlp:
                        act_low(t, c)

                if close:
                    add_mlp(t - 1)
                low(0)
                if close:
                    statistics(t - 1, 1, res2, res2_done, 2, stats2, stats2_done, moments2, moments2_done, norm2_step)
                low(1)
                low(2)
                if mix:
                    add_mix(t + 1)
                low(3)
                if mix:
                    statistics1(t + 1)
                low(4)
                if scores:
                    compare(t + 2)
                low(5)
                low(6)
                low(7)
                if scores:
                    masked_scores(t + 2)
                    x_low(t + 2)
                if close == "y":
                    add_input(t - 1)
                if mix:
                    h_low(t + 1)
                if scores:
                    invert_sums(t + 2)
                if dots:
                    token_dots(t + 3)
                if scores:
                    pt_low(t + 2)

            run_steps(dve, start, step, swap_weights=split_weights)

        @block.tensor
        def _(pe):
            def split_product(dst, products, done=None):
                last = None
                for n, (stationary, moving) in enumerate(products):
                    last = pe.matmul(dst, stationary, moving, start=(n == 0), stop=(n == len(products) - 1))
                if done is not None:
                    last.then_inc(done, 1)

            def spread_scores(u):
                pe.wait_ge(sj_done, u + 1)
                need(pe, neg_scores_done, u)
                for b in range(G):
                    split_product(ps_scores[:, b * N:(b + 1) * N],
                                  [(half[:, b:b + 1].broadcast_to([P, N]), neg_ident_r[:, :]) for half in (sj_hi, sj_lo)],
                                  scores_mm if b == G - 1 else None)

            def transpose_probs(u):
                pe.wait_ge(prob_done, G * u + G)
                need(pe, pt_done, u)
                for b in range(G):
                    last = pe.transpose(ps_pt[:, b * N:(b + 1) * N], prob[:, b * N:(b + 1) * N], ident[:, :])
                last.then_inc(pt_mm, 1)

            def mix_neighbours(u):
                pe.wait_ge(pt_done, u + 1)
                pe.wait_ge(x_lo_done, u + 1)
                need(pe, ht_hi_done, KD * u)
                need(pe, ht_done, KD * u)
                for b in range(G):
                    tok, feat = slice(b * N, (b + 1) * N), slice(b * D, (b + 1) * D)
                    split_product(ps_mix[:, b // 2, (b % 2) * D:(b % 2 + 1) * D],
                                  [(pt_hi[:, tok], x_hi[:, feat]), (pt_hi[:, tok], x_lo[:, feat]),
                                   (pt_lo[:, tok], x_hi[:, feat])],
                                  mix_mm if b % 2 else None)

            def transpose_z(u):
                pe.wait_ge(z1_done, G * u + G)
                pe.wait_ge(res1_done, G * u + G)
                for k in range(KD):
                    for b in range(G):
                        last = pe.transpose(ps_mix[:, k, b * N:(b + 1) * N], z1[:, b * D + k * P:b * D + (k + 1) * P],
                                            ident[:, :])
                    last.then_inc(zt_mm, 1)

            def first_product(u, c):
                if c == 0:
                    pe.wait_ge(ht_lo_done, u + 1)
                    pe.wait_ge(w1_split, layer(u) + 1)
                need(pe, gelu_done, KF * u + c - 1)
                cols = slice(c * P, (c + 1) * P)
                split_product(ps_hid[c % 2][:, :],
                              [(w[:, k, cols], h[:, k, :]) for w, h in ((w1_hi, ht_hi), (w1_lo, ht_hi), (w1_hi, ht_lo))
                               for k in range(KD)], hid_mm)

            def second_product(u, b):
                tok = slice(b * N, (b + 1) * N)
                dst = ps_mlp[:, b // 2, (b % 2) * D:(b % 2 + 1) * D]
                if b == 0:
                    pe.wait_ge(w2_split, layer(u) + 1)
                    need(pe, res2_done, 2 * u)
                for c in range(KF):
                    if b == 0:
                        pe.wait_ge(act_hi_done, KF * u + c + 1)
                    pe.matmul(dst, act_hi[:, c, tok], w2_hi[:, c, :], start=(c == 0), stop=False)
                    pe.matmul(dst, act_hi[:, c, tok], w2_lo[:, c, :], start=False, stop=False)
                for c in range(KF):
                    if b == 0:
                        pe.wait_ge(act_lo_done, KF * u + c + 1)
                    last = pe.matmul(dst, act_lo[:, c, tok], w2_hi[:, c, :], start=False, stop=(c == KF - 1))
                if b % 2:
                    last.then_inc(mlp_mm, 1)

            def start():
                pe.wait_ge(ident_done, 4)
                pe.wait_ge(neg_ident_done, 1)
                spread_scores(0)
                transpose_probs(0)
                mix_neighbours(0)
                transpose_z(0)
                spread_scores(1)
                transpose_probs(1)

            def step(t, close, dots=True, scores=True, mix=True, mlp=True):
                if mlp:
                    first_product(t, 0)
                    first_product(t, 1)
                if mix:
                    mix_neighbours(t + 1)
                if mlp:
                    for c in range(2, KF):
                        first_product(t, c)
                if scores:
                    spread_scores(t + 2)
                if mlp:
                    second_product(t, 0)
                if mix:
                    transpose_z(t + 1)
                if mlp:
                    second_product(t, 1)
                    second_product(t, 2)
                if scores:
                    transpose_probs(t + 2)
                if mlp:
                    second_product(t, 3)

            run_steps(pe, start, step)


_INS = ['x', 'adj', 'L0_gnn_attn_w', 'L0_gnn_attn_b', 'L0_gnn_W1', 'L0_gnn_b1', 'L0_gnn_W2', 'L0_gnn_b2',
        'L0_gnn_g1', 'L0_gnn_beta1', 'L0_gnn_g2', 'L0_gnn_beta2']
_OUTS = [((64, 128, 256), 'float32')]


def kernel(**inputs):
    import numpy as _np
    import concourse.bacc as _bacc
    from concourse import mybir as _mybir
    from concourse.bass_utils import run_bass_kernel_spmd as _run

    nc = _bacc.Bacc("TRN2", target_bir_lowering=False, num_devices=1, dynamic_dma_scratch_size=1024)
    arrays, args = {}, []
    for name in _INS:
        a = _np.ascontiguousarray(inputs[name])
        arrays[f"in_{name}_dram"] = a
        args.append(nc.dram_tensor(f"in_{name}_dram", a.shape, _mybir.dt.from_np(a.dtype), kind="ExternalInput").ap())
    for i, (shape, dtype) in enumerate(_OUTS):
        dt = _mybir.dt.from_np(_np.dtype(dtype))
        args.append(nc.dram_tensor(f"out_{i}_dram", shape, dt, kind="ExternalOutput").ap())
    gnn_layers_resnorm_kernel(nc, *args)
    r = _run(nc, [arrays], core_ids=[0])
    got = tuple(r.results[0][f"out_{i}_dram"] for i in range(len(_OUTS)))
    return got[0]
```

```python
from contextlib import ExitStack

import concourse.bass as bass
from concourse import mybir

ALU = mybir.AluOpType
ACT = mybir.ActivationFunctionType
F32 = mybir.dt.float32
F32R = mybir.dt.float32r
I32 = mybir.dt.int32
AX_X = mybir.AxisListType.X

P = 128
EPS = 1e-5
MASKED = 1e30
SLOPE = 0.2


def gnn_layers_resnorm_kernel(nc, x, adj, attn_w, attn_b, W1, b1, W2, b2, g1, beta1, g2, beta2, y_dram):
    B, N, D = x.shape
    L, _, F = W1.shape
    G = 4
    NG = B // G
    U = L * NG
    KD = D // P
    KF = F // P
    T = G * N
    GD = G * D
    assert N == P and T == 512 and NG == 16 and KD == 2 and KF == 8

    with ExitStack() as ctx:
        def sb(name, shape, dt=F32):
            return ctx.enter_context(nc.sbuf_tensor(name, shape, dt))

        def psum(name, shape):
            return ctx.enter_context(nc.psum_tensor(name, shape, F32))

        def sem(name):
            return ctx.enter_context(nc.semaphore(name))

        X = sb("X", [P, B * D])
        w1_raw = sb("w1_raw", [P, KD, F])
        w2_raw = sb("w2_raw", [P, KF, D])
        w1_hi = sb("w1_hi", [P, KD, F], F32R)
        w1_lo = sb("w1_lo", [P, KD, F], F32R)
        w2_hi = sb("w2_hi", [P, KF, D], F32R)
        w2_lo = sb("w2_lo", [P, KF, D], F32R)
        wi_rows = sb("wi_rows", [P, L, D])
        wj_rows = sb("wj_rows", [P, L, D])
        bias_attn = sb("bias_attn", [P, L])
        g1_rows = sb("g1_rows", [P, L, D])
        c1_rows = sb("c1_rows", [P, L, D])
        g2_rows = sb("g2_rows", [P, L, D])
        beta2_rows = sb("beta2_rows", [P, L, D])
        g1_cols = sb("g1_cols", [P, L, KD])
        beta1_cols = sb("beta1_cols", [P, L, KD])
        b1_cols = sb("b1_cols", [P, L, KF])
        b1_now = sb("b1_now", [P, KF])
        table_junk = sb("table_junk", [P, 1])
        ident = sb("ident", [P, P])
        neg_ident = sb("neg_ident", [P, P])
        neg_ident_r = sb("neg_ident_r", [P, P], F32R)
        minus_half = sb("minus_half", [P, G])
        adj_in = sb("adj_in", [P, T], I32)
        offset = sb("offset", [P, T])
        dot_junk = sb("dot_junk", [P, 2, D])
        si_raw = sb("si_raw", [P, G])
        neg_si = sb("neg_si", [P, G])
        sj = sb("sj", [P, G])
        sj_hi = sb("sj_hi", [P, G], F32R)
        sj_lo = sb("sj_lo", [P, G], F32R)
        neg_scores = sb("neg_scores", [P, T])
        neg_max = sb("neg_max", [P, G])
        prob = sb("prob", [P, T])
        row_sum = sb("row_sum", [P, G])
        row_inv = sb("row_inv", [P, G])
        pt_hi = sb("pt_hi", [P, T], F32R)
        pt_lo = sb("pt_lo", [P, T], F32R)
        x_hi = sb("x_hi", [P, GD], F32R)
        x_lo = sb("x_lo", [P, GD], F32R)
        res1 = sb("res1", [P, GD])
        stats1 = sb("stats1", [P, G, 6])
        moments1 = sb("moments1", [P, G, 2])
        scratch1 = sb("scratch1", [P, 4, G])
        z1 = sb("z1", [P, GD])
        q = sb("q", [P, GD])
        zt_hi = sb("zt_hi", [P, KD, T], F32R)
        zt_lo = sb("zt_lo", [P, KD, T], F32R)
        act_out = sb("act_out", [P, 4, T])
        act_hi = sb("act_hi", [P, KF, T], F32R)
        act_lo = sb("act_lo", [P, KF, T], F32R)
        res2 = sb("res2", [P, GD])
        stats2 = sb("stats2", [P, G, 6])
        moments2 = sb("moments2", [P, G, 2])
        scratch2 = sb("scratch2", [P, 4, G])
        y_slots = w2_raw[:, :, :].rearrange("p k d -> p (k d)")
        b2_rows = act_out[:, :, :].rearrange("p s t -> p (s t)")[:, 0:L * D].rearrange("p (l d) -> p l d", l=L)
        stats3 = sb("stats3", [P, G, 6])
        moments3 = sb("moments3", [P, G, 2])
        scratch3 = sb("scratch3", [P, 4, G])

        ps_mix = psum("ps_mix", [P, 2, T])
        ps_mlp = psum("ps_mlp", [P, 2, T])
        ps_hid = [psum("ps_hid0", [P, T]), psum("ps_hid1", [P, T])]
        ps_scores = psum("ps_scores", [P, T])
        ps_pt = psum("ps_pt", [P, T])

        params_in = sem("params_in")
        attn_in = sem("attn_in")
        x_in = [sem("x_in_0"), sem("x_in_1"), sem("x_in_2_3"), sem("x_in_rest")]
        adj_landed = sem("adj_landed")
        w1_in = sem("w1_in")
        w2_in = sem("w2_in")
        y_in = sem("y_in")
        stored = sem("stored")
        norm_const = sem("norm_const")
        neg_ident_done = sem("neg_ident_done")
        ident_done = sem("ident_done")
        w1_split = sem("w1_split")
        w1_hi_done = sem("w1_hi_done")
        w2_split = sem("w2_split")
        w2_hi_done = sem("w2_hi_done")
        c1_done = sem("c1_done")
        bias_mm = sem("bias_mm")
        b1_done = sem("b1_done")
        dots_done = sem("dots_done")
        sj_hi_done = sem("sj_hi_done")
        sj_done = sem("sj_done")
        neg_si_done = sem("neg_si_done")
        blocked_done = sem("blocked_done")
        offset_done = sem("offset_done")
        scores_mm = sem("scores_mm")
        neg_scores_done = sem("neg_scores_done")
        leaky_done = sem("leaky_done")
        neg_max_done = sem("neg_max_done")
        prob_done = sem("prob_done")
        row_inv_done = sem("row_inv_done")
        pt_mm = sem("pt_mm")
        pt_hi_done = sem("pt_hi_done")
        pt_done = sem("pt_done")
        x_hi_done = sem("x_hi_done")
        x_lo_done = sem("x_lo_done")
        mix_mm = sem("mix_mm")
        res1_done = sem("res1_done")
        stats1_done = sem("stats1_done")
        moments1_done = sem("moments1_done")
        norm1_step = sem("norm1_step")
        z1_done = sem("z1_done")
        q_step = sem("q_step")
        zt_mm = sem("zt_mm")
        zt_hi_done = sem("zt_hi_done")
        zt_lo_done = sem("zt_lo_done")
        hid_mm = sem("hid_mm")
        gelu_done = sem("gelu_done")
        act_hi_done = sem("act_hi_done")
        act_lo_done = sem("act_lo_done")
        mlp_mm = sem("mlp_mm")
        res2_done = sem("res2_done")
        stats2_done = sem("stats2_done")
        moments2_done = sem("moments2_done")
        norm2_step = sem("norm2_step")
        z2_done = sem("z2_done")
        x_scaled = sem("x_scaled")
        x_done = sem("x_done")
        res3_done = sem("res3_done")
        stats3_done = sem("stats3_done")
        moments3_done = sem("moments3_done")
        norm3_step = sem("norm3_step")
        y_done = sem("y_done")
        held = sem("held")

        LAST = (L - 1) * NG
        N_PARAMS = 5 + 2 * KD + L

        def group(u):
            return u % NG

        def layer(u):
            return u // NG

        def xg(u):
            return X[:, bass.ds(group(u) * GD, GD)]

        def xb(u, b):
            return X[:, bass.ds(group(u) * GD + b * D, D)]

        def row(params, u):
            return params[:, bass.ds(layer(u), 1), :].rearrange("p o d -> p (o d)")

        def rows4(params, u):
            return params[:, bass.ds(layer(u), 1), :].broadcast_to([P, G, D])

        def col(params, u, c):
            return params[:, bass.ds(layer(u), 1), c]

        def y_at(u, b=0, count=None):
            return y_slots[:, bass.ds((u % 2) * GD + b * D, count or GD)]

        def by_graph(ap):
            return ap.rearrange("p (b d) -> p b d", b=G)

        def need(eng, semaphore, value):
            if not isinstance(value, int) or value > 0:
                eng.wait_ge(semaphore, value)

        def hold(eng, semaphore, value):
            need(eng, semaphore, value)
            if not isinstance(value, int):
                eng.sem_inc(held, 1)

        def run_steps(eng, start, step):
            start()
            step(0, close=False)
            with eng.Fori(0, L - 1) as l:
                with eng.Fori(1, NG - 1) as g:
                    step(l * NG + g)
                step(l * NG + NG - 1, next_w1=l + 1)
                step(l * NG + NG, next_w2=l + 1)
            step(LAST + 1)
            step(LAST + 2, out=True)
            with eng.Fori(LAST + 3, U - 3) as t:
                step(t, out=True, write=True)
            step(U - 3, out=True, write=True, dots=False)
            step(U - 2, out=True, write=True, dots=False, scores=False)
            step(U - 1, out=True, write=True, dots=False, scores=False, mix=False)
            step(U, out=True, write=True, dots=False, scores=False, mix=False, mlp=False)
            step(U + 1, out=True, write=True, dots=False, scores=False, mix=False, mlp=False, close=False)
            step(U + 2, write=True, dots=False, scores=False, mix=False, mlp=False, close=False)

        ctx.enter_context(nc.allow_non_contiguous_dma(reason="3072 small parameters go down the partitions, once"))
        block = ctx.enter_context(nc.Block())

        def rows_of(src):
            return src.rearrange("(o l) d -> o l d", o=1).broadcast_to([P, L, src.shape[1]])

        @block.sync
        def _(sp):
            def load_x(g, count, landed):
                sp.dma_start(X[:, g * GD:(g + count) * GD].rearrange("p (b d) -> p b d", b=count * G),
                             x[g * G:(g + count) * G, :, :].rearrange("b i d -> i b d")).then_inc(landed, 16)

            def load_adj(u):
                need(sp, blocked_done, u)
                sp.dma_start(by_graph(adj_in[:, :]),
                             adj[bass.ds(group(u) * G, G), :, :].rearrange("b i j -> i b j")
                             ).then_inc(adj_landed, 16)

            def load_weights(l):
                need(sp, w1_split, KD * l)
                need(sp, bias_mm, l)
                sp.dma_start(w1_raw[:, :, :], W1[bass.ds(l, 1), :, :].rearrange("o (k p) f -> p (o k) f", p=P)
                             ).then_inc(w1_in, 16)
                need(sp, w2_split, l)
                sp.dma_start(w2_raw[:, :, :], W2[bass.ds(l, 1), :, :].rearrange("o (k p) d -> p (o k) d", p=P)
                             ).then_inc(w2_in, 16)

            def start():
                load_x(0, 1, x_in[0])
                sp.dma_start(wi_rows[:, :, :], rows_of(attn_w[:, 0:D])).then_inc(attn_in, 16)
                sp.dma_start(wj_rows[:, :, :], rows_of(attn_w[:, D:2 * D])).then_inc(attn_in, 16)
                sp.dma_start(bias_attn[:, :], attn_b.rearrange("(o l) -> o l", o=1).broadcast_to([P, L])
                             ).then_inc(attn_in, 16)
                load_adj(0)
                load_x(1, 1, x_in[1])
                load_x(2, 2, x_in[2])
                sp.wait_ge(adj_landed, 16)
                load_adj(1)
                load_x(4, NG - 4, x_in[3])
                sp.wait_ge(adj_landed, 32)

            def step(t, dots=True, scores=True, mix=True, mlp=True, close=True, out=False, write=False,
                     next_w1=None, next_w2=None):
                if scores:
                    load_adj(t + 2)
                if next_w1 is not None:
                    load_weights(next_w1)
                if out:
                    u = t - 2
                    sp.dma_start(by_graph(y_at(u)), x[bass.ds(group(u) * G, G), :, :].rearrange("b i d -> i b d")
                                 ).then_inc(y_in, 16)
                if scores:
                    hold(sp, adj_landed, 16 * t + 48)
                if out:
                    hold(sp, y_in, 16 * (u - LAST) + 16)
                if write:
                    u = t - 3
                    sp.wait_ge(y_done, G * (u - LAST) + G)
                    sp.dma_start(y_dram[bass.ds(group(u) * G, G), :, :].rearrange("b i d -> i b d"), by_graph(y_at(u))
                                 ).then_inc(stored, 16)
                    hold(sp, stored, 16 * (u - LAST) + 16)

            run_steps(sp, start, step)

        @block.gpsimd
        def _(pool):
            def offsets(u):
                pool.wait_ge(blocked_done, u + 1)
                hold(pool, neg_si_done, u + 1)
                for b in range(G):
                    pool.tensor_scalar(offset[:, b * N:(b + 1) * N], offset[:, b * N:(b + 1) * N], MASKED,
                                       neg_si[:, b:b + 1], ALU.mult, ALU.add).then_inc(offset_done, 1)

            def split_w2(l):
                pool.wait_ge(w2_in, 16 * l + 16)
                hold(pool, mlp_mm, l * (NG * 2))
                pool.tensor_scalar(w2_hi[:, :, :], w2_raw[:, :, :], 1.0, 0.0, ALU.mult, ALU.add
                                   ).then_inc(w2_hi_done, 1)
                pool.wait_ge(w2_hi_done, l + 1)
                pool.tensor_tensor(w2_lo[:, :, :], w2_raw[:, :, :], w2_hi[:, :, :].bitcast(F32), ALU.subtract
                                   ).then_inc(w2_split, 1)

            def scale_and_shift(n, first, moments_done, moments, scratch, norm_step, dst_done):
                var, rstd, nmean, shift = (scratch[:, i, :] for i in range(4))
                pool.wait_ge(moments_done, G * n + G + first)
                hold(pool, dst_done, G * n + first)
                pool.tensor_scalar(var, moments[:, :, 1], EPS, None, ALU.add).then_inc(norm_step, 1)
                pool.tensor_scalar(nmean, moments[:, :, 0], -1.0, None, ALU.mult).then_inc(norm_step, 1)
                pool.wait_ge(norm_step, 4 * n + 2 + first)
                pool.tensor_tensor(rstd, var, minus_half[:, :], ALU.pow).then_inc(norm_step, 1)
                pool.wait_ge(norm_step, 4 * n + 3 + first)
                pool.tensor_tensor(shift, nmean, rstd, ALU.mult).then_inc(norm_step, 1)

            def normalise(n, first, moments_done, moments, scratch, norm_step, src, dst, dst_done):
                scale_and_shift(n, first, moments_done, moments, scratch, norm_step, dst_done)
                rstd, shift = scratch[:, 1, :], scratch[:, 3, :]
                hold(pool, norm_step, 4 * n + 4 + first)
                for b in range(G):
                    pool.tensor_scalar(dst[:, b * D:(b + 1) * D], src[:, b * D:(b + 1) * D], rstd[:, b:b + 1],
                                       shift[:, b:b + 1], ALU.mult, ALU.add).then_inc(dst_done, 1)

            def normalise1(u):
                need(pool, zt_mm, u)
                need(pool, q_step, 2 * u)
                normalise(u, 0, moments1_done, moments1, scratch1, norm1_step, res1, z1, z1_done)

            def residual1(u):
                pool.wait_ge(z1_done, G * u + G)
                pool.wait_ge(c1_done, 1)
                hold(pool, res2_done, 2 * u)
                pool.tensor_tensor(by_graph(q[:, :]), by_graph(z1[:, :]), rows4(g1_rows, u), ALU.mult
                                   ).then_inc(q_step, 1)
                hold(pool, q_step, 2 * u + 1)
                pool.tensor_tensor(by_graph(q[:, :]), by_graph(q[:, :]), rows4(c1_rows, u), ALU.add
                                   ).then_inc(q_step, 1)

            def normalise2(u):
                pool.wait_ge(x_done, u + 1)
                normalise(u, 1, moments2_done, moments2, scratch2, norm2_step, res2, res2, z2_done)

            def update_x(u):
                hold(pool, z2_done, G * u + G + 1)
                pool.tensor_tensor(by_graph(xg(u)), by_graph(res2[:, :]), rows4(g2_rows, u), ALU.mult
                                   ).then_inc(x_scaled, 1)
                hold(pool, x_scaled, u + 2)
                pool.tensor_tensor(by_graph(xg(u)), by_graph(xg(u)), rows4(beta2_rows, u), ALU.add
                                   ).then_inc(x_done, 1)

            def start():
                for tile in (ident, neg_ident):
                    pool.memset(tile[:, :], 0.0).then_inc(ident_done, 1)
                pool.memset(minus_half[:, :], -0.5).then_inc(norm_const, 1)
                for i, free in enumerate((z2_done, x_scaled, x_done)):
                    pool.memset(res2[:, i:i + 1], 0.0).then_inc(free, 1)
                pool.memset(scratch2[:, 0, 0:1], 0.0).then_inc(norm2_step, 1)
                pool.wait_ge(ident_done, 2)
                for tile, fill in ((ident, 1.0), (neg_ident, -1.0)):
                    pool.affine_select(out=tile[:, :], in_=tile[:, :], compare_op=ALU.not_equal, fill=fill, base=0,
                                       pattern=[[-1, P]], channel_multiplier=1).then_inc(ident_done, 1)
                pool.wait_ge(norm_const, 1)
                offsets(0)
                offsets(1)
                normalise1(0)
                pool.wait_ge(params_in, 16 * N_PARAMS)
                pool.tensor_tensor(c1_rows[:, :, :], c1_rows[:, :, :], b2_rows, ALU.add).then_inc(c1_done, 1)
                split_w2(0)

            def step(t, dots=True, scores=True, mix=True, mlp=True, close=True, out=False, write=False,
                     next_w1=None, next_w2=None):
                if next_w2 is not None:
                    split_w2(next_w2)
                if mlp:
                    residual1(t)
                if scores:
                    offsets(t + 2)
                if mix:
                    normalise1(t + 1)
                if close:
                    normalise2(t - 1)
                    update_x(t - 1)
                if out:
                    scale_and_shift(t - 2 - LAST, 0, moments3_done, moments3, scratch3, norm3_step, y_done)

            run_steps(pool, start, step)

        @block.scalar
        def _(act):
            def split_w1(l):
                act.wait_ge(w1_in, 16 * l + 16)
                need(act, hid_mm, l * (NG * KF))
                for k in range(KD):
                    act.activation(w1_hi[:, k, :], w1_raw[:, k, :], ACT.Copy, scale=g1_cols[:, bass.ds(l, 1), k]
                                   ).then_inc(w1_hi_done, 1)

            def x_high(u):
                need(act, mix_mm, 2 * u)
                need(act, x_lo_done, u)
                act.activation(x_hi[:, :], xg(u), ACT.Copy).then_inc(x_hi_done, 1)

            def softmax_numerators(u):
                act.wait_ge(neg_max_done, u + 1)
                need(act, pt_mm, u)
                need(act, row_inv_done, u)
                for b in range(G):
                    act.activation(prob[:, b * N:(b + 1) * N], neg_scores[:, b * N:(b + 1) * N], ACT.Exp,
                                   bias=neg_max[:, b:b + 1], scale=-1.0, accum_out=row_sum[:, b:b + 1]
                                   ).then_inc(prob_done, 1)

            def pt_high(u):
                act.wait_ge(pt_mm, u + 1)
                need(act, mix_mm, 2 * u)
                need(act, pt_done, u)
                act.activation(pt_hi[:, :], ps_pt[:, :], ACT.Copy).then_inc(pt_hi_done, 1)

            def z_high(u):
                act.wait_ge(zt_mm, u + 1)
                need(act, hid_mm, KF * u)
                need(act, zt_lo_done, u)
                act.activation(zt_hi[:, :, :], ps_mix[:, :, :], ACT.Copy).then_inc(zt_hi_done, 1)

            def gelu(u, c):
                act.wait_ge(hid_mm, KF * u + c + 1)
                if c == 0:
                    act.wait_ge(b1_done, layer(u) + 1)
                    need(act, mlp_mm, 2 * u)
                need(act, act_lo_done, KF * u + c - 3)
                for dst, done in ((act_out[:, c % 4, :], gelu_done), (act_hi[:, c, :], act_hi_done)):
                    act.activation(dst, ps_hid[c % 2][:, :], ACT.Gelu, bias=b1_now[:, c:c + 1]).then_inc(done, 1)

            def load_table(func):
                act.activation(table_junk[:, 0:1], ident[:, 0:1], func)

            def normalise_y(u):
                n = u - LAST
                act.wait_ge(norm3_step, 4 * n + 4)
                for b in range(G):
                    act.activation(y_at(u, b, D), y_at(u, b, D), ACT.Identity,
                                   bias=scratch3[:, 3, b:b + 1], scale=scratch3[:, 1, b:b + 1]).then_inc(y_done, 1)

            def start():
                def param(dst, src):
                    act.dma_start(dst, src).then_inc(params_in, 16)

                act.dma_start(w1_raw[:, :, :], W1[0, :, :].rearrange("(k p) f -> p k f", p=P)).then_inc(w1_in, 16)
                for k in range(KD):
                    param(g1_cols[:, :, k], g1[:, k * P:(k + 1) * P].rearrange("l p -> p l"))
                    param(beta1_cols[:, :, k], beta1[:, k * P:(k + 1) * P].rearrange("l p -> p l"))
                for l in range(L):
                    param(b1_cols[:, l, :], b1[l, :].rearrange("(k p) -> p k", p=P))
                act.wait_ge(ident_done, 4)
                act.wait_ge(x_in[0], 16)
                x_high(0)
                for tile, src in ((g1_rows, g1), (c1_rows, beta1), (g2_rows, g2), (beta2_rows, beta2)):
                    param(tile[:, :, :], rows_of(src))
                param(b2_rows, rows_of(b2))
                act.dma_start(w2_raw[:, :, :], W2[0, :, :].rearrange("(k p) d -> p k d", p=P)).then_inc(w2_in, 16)
                softmax_numerators(0)
                pt_high(0)
                softmax_numerators(1)
                act.wait_ge(params_in, 16 * N_PARAMS)
                split_w1(0)
                act.wait_ge(x_in[1], 16)
                x_high(1)
                pt_high(1)
                z_high(0)
                load_table(ACT.Gelu)
                act.wait_ge(c1_done, 1)

            def step(t, dots=True, scores=True, mix=True, mlp=True, close=True, out=False, write=False,
                     next_w1=None, next_w2=None):
                if mlp:
                    for c in range(KF):
                        gelu(t, c)
                if scores:
                    x_high(t + 2)
                    softmax_numerators(t + 2)
                if mix:
                    z_high(t + 1)
                if next_w1 is not None:
                    split_w1(next_w1)
                if scores:
                    pt_high(t + 2)
                if write:
                    normalise_y(t - 3)
                if mix:
                    load_table(ACT.Gelu)

            run_steps(act, start, step)

        @block.vector
        def _(dve):
            def split_w1(l):
                dve.wait_ge(w1_hi_done, KD * l + KD)
                need(dve, hid_mm, l * (NG * KF))
                for k in range(KD):
                    dve.scalar_tensor_tensor(w1_lo[:, k, :], w1_raw[:, k, :], g1_cols[:, bass.ds(l, 1), k],
                                             w1_hi[:, k, :].bitcast(F32), ALU.mult, ALU.subtract
                                             ).then_inc(w1_split, 1)
                dve.wait_ge(bias_mm, l + 1)
                need(dve, act_hi_done, l * (NG * KF))
                dve.tensor_tensor(b1_now[:, :], ps_hid[0][:, 0:KF], b1_cols[:, bass.ds(l, 1), :].rearrange("p o c -> p (o c)"),
                                  ALU.add).then_inc(b1_done, 1)

            def token_dots(u):
                dve.wait_ge(x_in[0 if isinstance(u, int) and u == 0 else 1 if isinstance(u, int) and u == 1 else
                                 2 if isinstance(u, int) and u < 4 else 3], 16)
                need(dve, neg_si_done, u)
                need(dve, sj_done, u)
                for n in range(2 * G):
                    b = n % G
                    sign, weights, dot = (-1.0, wi_rows, si_raw) if n < G else (1.0, wj_rows, sj)
                    need(dve, dots_done, 2 * G * u + n - 1)
                    dve.scalar_tensor_tensor(dot_junk[:, n % 2, :], xb(u, b), sign, row(weights, u), ALU.mult,
                                             ALU.mult, accum_out=dot[:, b:b + 1]).then_inc(dots_done, 1)
                dve.wait_ge(dots_done, 2 * G * u + G)
                need(dve, offset_done, G * u)
                dve.tensor_scalar(neg_si[:, :], si_raw[:, :], bias_attn[:, bass.ds(layer(u), 1)], None, ALU.subtract
                                  ).then_inc(neg_si_done, 1)
                dve.wait_ge(dots_done, 2 * G * u + 2 * G)
                need(dve, scores_mm, u)
                dve.tensor_copy(sj_hi[:, :], sj[:, :]).then_inc(sj_hi_done, 1)
                dve.wait_ge(sj_hi_done, u + 1)
                dve.tensor_tensor(sj_lo[:, :], sj[:, :], sj_hi[:, :].bitcast(F32), ALU.subtract).then_inc(sj_done, 1)

            def compare(u):
                dve.wait_ge(adj_landed, 16 * u + 16)
                need(dve, neg_scores_done, u)
                dve.tensor_tensor(by_graph(offset[:, :]), by_graph(adj_in[:, :]),
                                  neg_ident[:, :].unsqueeze(1).broadcast_to([P, G, N]), ALU.is_le
                                  ).then_inc(blocked_done, 1)

            def masked_scores(u):
                dve.wait_ge(scores_mm, u + 1)
                dve.wait_ge(offset_done, G * u + G)
                need(dve, prob_done, G * u)
                dve.tensor_tensor(neg_scores[:, :], ps_scores[:, :], offset[:, :], ALU.add).then_inc(neg_scores_done, 1)
                dve.wait_ge(neg_scores_done, u + 1)
                dve.scalar_tensor_tensor(neg_scores[:, :], neg_scores[:, :], SLOPE, neg_scores[:, :], ALU.mult, ALU.min
                                         ).then_inc(leaky_done, 1)
                dve.wait_ge(leaky_done, u + 1)
                dve.tensor_reduce(neg_max[:, :], by_graph(neg_scores[:, :]), AX_X, ALU.min).then_inc(neg_max_done, 1)

            def invert_sums(u):
                dve.wait_ge(prob_done, G * u + G)
                need(dve, res1_done, G * u)
                dve.reciprocal(row_inv[:, :], row_sum[:, :]).then_inc(row_inv_done, 1)

            def x_low(u):
                dve.wait_ge(x_hi_done, u + 1)
                need(dve, mix_mm, 2 * u)
                dve.tensor_tensor(x_lo[:, :], xg(u), x_hi[:, :].bitcast(F32), ALU.subtract).then_inc(x_lo_done, 1)

            def pt_low(u):
                dve.wait_ge(pt_hi_done, u + 1)
                need(dve, mix_mm, 2 * u)
                dve.tensor_tensor(pt_lo[:, :], ps_pt[:, :], pt_hi[:, :].bitcast(F32), ALU.subtract).then_inc(pt_done, 1)

            def add_mix(u):
                dve.wait_ge(row_inv_done, u + 1)
                need(dve, z1_done, G * u)
                for b in range(G):
                    if b % 2 == 0:
                        dve.wait_ge(mix_mm, 2 * u + b // 2 + 1)
                    dve.scalar_tensor_tensor(res1[:, b * D:(b + 1) * D], ps_mix[:, b // 2, (b % 2) * D:(b % 2 + 1) * D],
                                             row_inv[:, b:b + 1], xb(u, b), ALU.mult, ALU.add).then_inc(res1_done, 1)

            def statistics(n, first, src, src_done, per_src, stats, stats_done, moments, moments_done, norm_step):
                need(dve, moments_done, G * n + first)
                for b in range(G):
                    if b % (G // per_src) == 0:
                        (hold if per_src == 1 else need)(dve, src_done, per_src * n + b // (G // per_src) + 1)
                    dve.bn_stats(stats[:, b, :], src(b)).then_inc(stats_done, 1)
                need(dve, norm_step, 4 * n + first)
                hold(dve, stats_done, G * n + G)
                for b in range(G):
                    dve.bn_aggr(moments[:, b, :], stats[:, b, :]).then_inc(moments_done, 1)

            def statistics1(u):
                statistics(u, 0, (lambda b: res1[:, b * D:(b + 1) * D]), res1_done, G, stats1, stats1_done, moments1, moments1_done, norm1_step)

            def z_low(u):
                dve.wait_ge(zt_hi_done, u + 1)
                need(dve, hid_mm, KF * u)
                dve.tensor_tensor(zt_lo[:, :, :], ps_mix[:, :, :], zt_hi[:, :, :].bitcast(F32), ALU.subtract
                                  ).then_inc(zt_lo_done, 1)

            def act_low(u, c):
                dve.wait_ge(gelu_done, KF * u + c + 1)
                dve.wait_ge(act_hi_done, KF * u + c + 1)
                if c == 0:
                    need(dve, mlp_mm, 2 * u)
                dve.tensor_tensor(act_lo[:, c, :], act_out[:, c % 4, :], act_hi[:, c, :].bitcast(F32), ALU.subtract
                                  ).then_inc(act_lo_done, 1)

            def add_mlp(u):
                dve.wait_ge(q_step, 2 * u + 2)
                dve.wait_ge(z2_done, G * u + 1)
                dve.wait_ge(x_scaled, u + 1)
                for i in range(2):
                    dve.wait_ge(mlp_mm, 2 * u + i + 1)
                    dve.tensor_tensor(res2[:, i * T:(i + 1) * T], ps_mlp[:, i, :], q[:, i * T:(i + 1) * T], ALU.add
                                      ).then_inc(res2_done, 1)

            def add_input(u):
                n = u - LAST
                dve.wait_ge(x_done, u + 2)
                dve.wait_ge(y_in, 16 * n + 16)
                dve.tensor_tensor(y_at(u), xg(u), y_at(u), ALU.add).then_inc(res3_done, 1)
                statistics(n, 0, (lambda b: y_at(u, b, D)), res3_done, 1, stats3, stats3_done, moments3, moments3_done, norm3_step)

            def start():
                dve.memset(moments2[:, :, :], 0.0).then_inc(moments2_done, 1)
                dve.wait_ge(ident_done, 4)
                dve.tensor_copy(neg_ident_r[:, :], neg_ident[:, :]).then_inc(neg_ident_done, 1)
                dve.wait_ge(attn_in, 48)
                token_dots(0)
                compare(0)
                masked_scores(0)
                x_low(0)
                token_dots(1)
                compare(1)
                invert_sums(0)
                pt_low(0)
                masked_scores(1)
                add_mix(0)
                statistics1(0)
                invert_sums(1)
                x_low(1)
                dve.wait_ge(params_in, 16 * N_PARAMS)
                split_w1(0)
                pt_low(1)
                z_low(0)
                token_dots(2)

            def step(t, dots=True, scores=True, mix=True, mlp=True, close=True, out=False, write=False,
                     next_w1=None, next_w2=None):
                def low(c):
                    if mlp:
                        act_low(t, c)

                if close:
                    add_mlp(t - 1)
                    statistics(t - 1, 1, (lambda b: res2[:, b * D:(b + 1) * D]), res2_done, 2, stats2, stats2_done,
                               moments2, moments2_done, norm2_step)
                low(0)
                if scores:
                    compare(t + 2)
                low(1)
                if mix:
                    add_mix(t + 1)
                low(2)
                low(3)
                if mix:
                    statistics1(t + 1)
                for c in range(4, KF):
                    low(c)
                if scores:
                    masked_scores(t + 2)
                    x_low(t + 2)
                if mix:
                    z_low(t + 1)
                if next_w1 is not None:
                    split_w1(next_w1)
                if scores:
                    invert_sums(t + 2)
                if dots:
                    token_dots(t + 3)
                if scores:
                    pt_low(t + 2)
                if out:
                    add_input(t - 2)

            run_steps(dve, start, step)

        @block.tensor
        def _(pe):
            def split_product(dst, products, done=None):
                last = None
                for n, (stationary, moving) in enumerate(products):
                    last = pe.matmul(dst, stationary, moving, start=(n == 0), stop=(n == len(products) - 1))
                if done is not None:
                    last.then_inc(done, 1)

            def spread_scores(u):
                pe.wait_ge(sj_done, u + 1)
                need(pe, neg_scores_done, u)
                for b in range(G):
                    split_product(ps_scores[:, b * N:(b + 1) * N],
                                  [(half[:, b:b + 1].broadcast_to([P, N]), neg_ident_r[:, :]) for half in (sj_hi, sj_lo)],
                                  scores_mm if b == G - 1 else None)

            def transpose_probs(u):
                pe.wait_ge(prob_done, G * u + G)
                need(pe, pt_done, u)
                for b in range(G):
                    last = pe.transpose(ps_pt[:, b * N:(b + 1) * N], prob[:, b * N:(b + 1) * N], ident[:, :])
                last.then_inc(pt_mm, 1)

            def mix_neighbours(u):
                pe.wait_ge(pt_done, u + 1)
                pe.wait_ge(x_lo_done, u + 1)
                need(pe, zt_lo_done, u)
                for b in range(G):
                    tok, feat = slice(b * N, (b + 1) * N), slice(b * D, (b + 1) * D)
                    split_product(ps_mix[:, b // 2, (b % 2) * D:(b % 2 + 1) * D],
                                  [(pt_hi[:, tok], x_hi[:, feat]), (pt_hi[:, tok], x_lo[:, feat]),
                                   (pt_lo[:, tok], x_hi[:, feat])],
                                  mix_mm if b % 2 else None)

            def transpose_z(u):
                pe.wait_ge(z1_done, G * u + G)
                pe.wait_ge(res1_done, G * u + G)
                for k in range(KD):
                    for b in range(G):
                        last = pe.transpose(ps_mix[:, k, b * N:(b + 1) * N], z1[:, b * D + k * P:b * D + (k + 1) * P],
                                            ident[:, :])
                last.then_inc(zt_mm, 1)

            def bias_product(l):
                pe.wait_ge(w1_in, 16 * l + 16)
                need(pe, act_hi_done, l * (NG * KF))
                for c in range(KF):
                    for k in range(KD):
                        last = pe.matmul(ps_hid[0][:, c:c + 1], w1_raw[:, k, c * P:(c + 1) * P],
                                         beta1_cols[:, bass.ds(l, 1), k], start=(k == 0), stop=(k == KD - 1))
                last.then_inc(bias_mm, 1)

            def first_product(u, c):
                cols = slice(c * P, (c + 1) * P)
                dst = ps_hid[c % 2][:, :]
                if c == 0:
                    pe.wait_ge(w1_split, KD * layer(u) + KD)
                    pe.wait_ge(zt_hi_done, u + 1)
                    pe.wait_ge(b1_done, layer(u) + 1)
                need(pe, act_hi_done, KF * u + c - 1)
                for n, w in enumerate((w1_hi, w1_lo)):
                    for k in range(KD):
                        pe.matmul(dst, w[:, k, cols], zt_hi[:, k, :], start=(n + k == 0), stop=False)
                if c == 0:
                    pe.wait_ge(zt_lo_done, u + 1)
                for k in range(KD):
                    last = pe.matmul(dst, w1_hi[:, k, cols], zt_lo[:, k, :], start=False, stop=(k == KD - 1))
                last.then_inc(hid_mm, 1)

            def second_product(u, b):
                tok = slice(b * N, (b + 1) * N)
                dst = ps_mlp[:, b // 2, (b % 2) * D:(b % 2 + 1) * D]
                if b == 0:
                    pe.wait_ge(w2_split, layer(u) + 1)
                    need(pe, res2_done, 2 * u)
                for c in range(KF):
                    if b == 0:
                        pe.wait_ge(act_hi_done, KF * u + c + 1)
                    pe.matmul(dst, act_hi[:, c, tok], w2_hi[:, c, :], start=(c == 0), stop=False)
                    pe.matmul(dst, act_hi[:, c, tok], w2_lo[:, c, :], start=False, stop=False)
                for c in range(KF):
                    if b == 0:
                        pe.wait_ge(act_lo_done, KF * u + c + 1)
                    last = pe.matmul(dst, act_lo[:, c, tok], w2_hi[:, c, :], start=False, stop=(c == KF - 1))
                if b % 2:
                    last.then_inc(mlp_mm, 1)

            def start():
                pe.wait_ge(ident_done, 4)
                pe.wait_ge(neg_ident_done, 1)
                spread_scores(0)
                transpose_probs(0)
                spread_scores(1)
                mix_neighbours(0)
                pe.wait_ge(params_in, 16 * N_PARAMS)
                bias_product(0)
                transpose_probs(1)
                transpose_z(0)

            def step(t, dots=True, scores=True, mix=True, mlp=True, close=True, out=False, write=False,
                     next_w1=None, next_w2=None):
                if mlp:
                    first_product(t, 0)
                    first_product(t, 1)
                if mix:
                    mix_neighbours(t + 1)
                if mlp:
                    for c in range(2, KF):
                        first_product(t, c)
                if scores:
                    spread_scores(t + 2)
                if mlp:
                    second_product(t, 0)
                if mix:
                    transpose_z(t + 1)
                if next_w1 is not None:
                    bias_product(next_w1)
                if mlp:
                    second_product(t, 1)
                    second_product(t, 2)
                if scores:
                    transpose_probs(t + 2)
                if mlp:
                    second_product(t, 3)

            run_steps(pe, start, step)


_INS = ['x', 'adj', 'L0_gnn_attn_w', 'L0_gnn_attn_b', 'L0_gnn_W1', 'L0_gnn_b1', 'L0_gnn_W2', 'L0_gnn_b2',
        'L0_gnn_g1', 'L0_gnn_beta1', 'L0_gnn_g2', 'L0_gnn_beta2']
_OUTS = [((64, 128, 256), 'float32')]


def kernel(**inputs):
    import numpy as _np
    import concourse.bacc as _bacc
    from concourse import mybir as _mybir
    from concourse.bass_utils import run_bass_kernel_spmd as _run

    nc = _bacc.Bacc("TRN2", target_bir_lowering=False, num_devices=1, dynamic_dma_scratch_size=1024)
    arrays, args = {}, []
    for name in _INS:
        a = _np.ascontiguousarray(inputs[name])
        arrays[f"in_{name}_dram"] = a
        args.append(nc.dram_tensor(f"in_{name}_dram", a.shape, _mybir.dt.from_np(a.dtype), kind="ExternalInput").ap())
    for i, (shape, dtype) in enumerate(_OUTS):
        dt = _mybir.dt.from_np(_np.dtype(dtype))
        args.append(nc.dram_tensor(f"out_{i}_dram", shape, dt, kind="ExternalOutput").ap())
    gnn_layers_resnorm_kernel(nc, *args)
    r = _run(nc, [arrays], core_ids=[0])
    got = tuple(r.results[0][f"out_{i}_dram"] for i in range(len(_OUTS)))
    return got[0]
```

```python
from contextlib import ExitStack

import concourse.bass as bass
from concourse import mybir

ALU = mybir.AluOpType
ACT = mybir.ActivationFunctionType
F32 = mybir.dt.float32
F32R = mybir.dt.float32r
I32 = mybir.dt.int32
AX_X = mybir.AxisListType.X

P = 128
EPS = 1e-5
MASKED = 1e30
SLOPE = 0.2


def gnn_layers_resnorm_kernel(nc, x, adj, attn_w, attn_b, W1, b1, W2, b2, g1, beta1, g2, beta2, y_dram):
    B, N, D = x.shape
    L, _, F = W1.shape
    G = 4
    NG = B // G
    U = L * NG
    KD = D // P
    KF = F // P
    T = G * N
    GD = G * D
    assert N == P and T == 512 and NG == 16 and KD == 2 and KF == 8

    with ExitStack() as ctx:
        def sb(name, shape, dt=F32):
            return ctx.enter_context(nc.sbuf_tensor(name, shape, dt))

        def psum(name, shape):
            return ctx.enter_context(nc.psum_tensor(name, shape, F32))

        def sem(name):
            return ctx.enter_context(nc.semaphore(name))

        X = sb("X", [P, B * D])
        w1_raw = sb("w1_raw", [P, KD, F])
        w2_raw = sb("w2_raw", [P, KF, D])
        w1_hi = sb("w1_hi", [P, KD, F], F32R)
        w1_lo = sb("w1_lo", [P, KD, F], F32R)
        w2_hi = sb("w2_hi", [P, KF, D], F32R)
        w2_lo = sb("w2_lo", [P, KF, D], F32R)
        wi_rows = sb("wi_rows", [P, L, D])
        wj_rows = sb("wj_rows", [P, L, D])
        bias_attn = sb("bias_attn", [P, L])
        g1_rows = sb("g1_rows", [P, L, D])
        c1_rows = sb("c1_rows", [P, L, D])
        b2_rows = sb("b2_rows", [P, L, D])
        g2_rows = sb("g2_rows", [P, L, D])
        beta2_rows = sb("beta2_rows", [P, L, D])
        g1_cols = sb("g1_cols", [P, L, KD])
        beta1_cols = sb("beta1_cols", [P, L, KD])
        b1_cols = sb("b1_cols", [P, L, KF])
        table_junk = sb("table_junk", [P, 1])
        ident = sb("ident", [P, P])
        neg_ident = sb("neg_ident", [P, P])
        minus_half = sb("minus_half", [P, G])
        adj_in = sb("adj_in", [P, T], I32)
        adj_second = sb("adj_second", [P, T], I32)
        offset = sb("offset", [P, T])
        dot_junk = sb("dot_junk", [P, 2, D])
        si_raw = sb("si_raw", [P, G])
        neg_si = sb("neg_si", [P, G])
        neg_sj = sb("neg_sj", [P, G])
        neg_scores = sb("neg_scores", [P, T])
        neg_max = sb("neg_max", [P, G])
        prob = sb("prob", [P, T])
        row_sum = sb("row_sum", [P, G])
        row_inv = sb("row_inv", [P, G])
        pt_hi = sb("pt_hi", [P, T], F32R)
        pt_lo = sb("pt_lo", [P, T], F32R)
        x_hi = sb("x_hi", [P, GD], F32R)
        x_lo = sb("x_lo", [P, GD], F32R)
        res1 = sb("res1", [P, GD])
        stats1 = sb("stats1", [P, G, 6])
        moments1 = sb("moments1", [P, G, 2])
        scratch1 = sb("scratch1", [P, 4, G])
        z1 = sb("z1", [P, GD])
        q = sb("q", [P, GD])
        ht_hi = sb("ht_hi", [P, KD, T], F32R)
        ht_lo = sb("ht_lo", [P, KD, T], F32R)
        act_hi = sb("act_hi", [P, KF, T], F32R)
        act_lo = sb("act_lo", [P, KF, T], F32R)
        res2 = sb("res2", [P, GD])
        stats2 = sb("stats2", [P, G, 6])
        moments2 = sb("moments2", [P, G, 2])
        scratch2 = sb("scratch2", [P, 4, G])
        x_input = w2_raw[:, 0:G, :].rearrange("p b d -> p (b d)")
        y = w2_raw[:, G:2 * G, :].rearrange("p b d -> p (b d)")
        stats3 = sb("stats3", [P, G, 6])
        moments3 = sb("moments3", [P, G, 2])
        scratch3 = sb("scratch3", [P, 4, G])

        ps_mix = psum("ps_mix", [P, 2, T])
        ps_mlp = psum("ps_mlp", [P, 2, T])
        ps_hid = [psum(f"ps_hid{i}", [P, T]) for i in range(3)]
        ps_scores = psum("ps_scores", [P, T])

        cols_in = sem("cols_in")
        rows_in = sem("rows_in")
        attn_in = sem("attn_in")
        x_in = [sem("x_in_0"), sem("x_in_1"), sem("x_in_2_3"), sem("x_in_rest")]
        adj_landed = sem("adj_landed")
        adj_second_in = sem("adj_second_in")
        w1_in = sem("w1_in")
        w2_in = sem("w2_in")
        y_in = sem("y_in")
        stored = sem("stored")
        norm_const = sem("norm_const")
        ident_done = sem("ident_done")
        w1_split = sem("w1_split")
        w1_hi_done = sem("w1_hi_done")
        w2_split = sem("w2_split")
        w2_hi_done = sem("w2_hi_done")
        c1_done = sem("c1_done")
        dots_done = sem("dots_done")
        neg_si_done = sem("neg_si_done")
        blocked_done = sem("blocked_done")
        offset_done = sem("offset_done")
        scores_mm = sem("scores_mm")
        neg_scores_done = sem("neg_scores_done")
        leaky_done = sem("leaky_done")
        neg_max_done = sem("neg_max_done")
        prob_done = sem("prob_done")
        row_inv_done = sem("row_inv_done")
        pt_mm = sem("pt_mm")
        pt_hi_done = sem("pt_hi_done")
        pt_done = sem("pt_done")
        x_hi_done = sem("x_hi_done")
        x_lo_done = sem("x_lo_done")
        mix_mm = sem("mix_mm")
        res1_done = sem("res1_done")
        stats1_done = sem("stats1_done")
        moments1_done = sem("moments1_done")
        norm1_step = sem("norm1_step")
        z1_done = sem("z1_done")
        q_step = sem("q_step")
        zt_mm = sem("zt_mm")
        ht_step = sem("ht_step")
        ht_hi_done = sem("ht_hi_done")
        ht_lo_done = sem("ht_lo_done")
        hid_mm = sem("hid_mm")
        gelu_done = sem("gelu_done")
        act_hi_done = sem("act_hi_done")
        act_lo_done = sem("act_lo_done")
        mlp_mm = sem("mlp_mm")
        res2_done = sem("res2_done")
        stats2_done = sem("stats2_done")
        moments2_done = sem("moments2_done")
        norm2_step = sem("norm2_step")
        z2_done = sem("z2_done")
        x_step = sem("x_step")
        last_input_in = sem("last_input_in")
        last_input_done = sem("last_input_done")
        last_scaled = sem("last_scaled")
        last_y_done = [sem("last_y_done_0"), sem("last_y_done_1")]
        res3_done = sem("res3_done")
        stats3_done = sem("stats3_done")
        moments3_done = sem("moments3_done")
        norm3_step = sem("norm3_step")
        y_done = sem("y_done")
        held = sem("held")

        LAST = (L - 1) * NG
        N_ROWS = 5
        N_COLS = 2 * KD + L

        def group(u):
            return u % NG

        def layer(u):
            return u // NG

        def xg(u):
            return X[:, bass.ds(group(u) * GD, GD)]

        def xb(u, b):
            return X[:, bass.ds(group(u) * GD + b * D, D)]

        def row(params, u):
            return params[:, bass.ds(layer(u), 1), :].rearrange("p o d -> p (o d)")

        def rows4(params, u):
            return params[:, bass.ds(layer(u), 1), :].broadcast_to([P, G, D])

        def col(params, u, c):
            return params[:, bass.ds(layer(u), 1), c]

        def by_graph(ap):
            return ap.rearrange("p (b d) -> p b d", b=G)

        def need(eng, semaphore, value):
            if not isinstance(value, int) or value > 0:
                eng.wait_ge(semaphore, value)

        def hold(eng, semaphore, value):
            need(eng, semaphore, value)
            if not isinstance(value, int):
                eng.sem_inc(held, 1)

        def run_steps(eng, start, step, finish):
            start()
            step(0, close=False)
            with eng.Fori(0, L - 1) as l:
                with eng.Fori(1, NG - 1) as g:
                    step(l * NG + g)
                step(l * NG + NG - 1, next_w1=l + 1)
                step(l * NG + NG, next_w2=l + 1)
            step(LAST + 1)
            step(LAST + 2, out=True)
            with eng.Fori(LAST + 3, U - 3) as t:
                step(t, out=True, write=True)
            step(U - 3, out=True, write=True, dots=False)
            step(U - 2, out=True, write=True, dots=False, scores=False)
            step(U - 1, out=True, write=True, before_last=True, dots=False, scores=False, mix=False)
            step(U, out=True, write=True, update=False, dots=False, scores=False, mix=False, mlp=False)
            step(U + 1, write=True, dots=False, scores=False, mix=False, mlp=False, close=False)
            finish()

        def scale_x(eng, u):
            hold(eng, z2_done, G * u + G + 1)
            eng.tensor_tensor(by_graph(xg(u)), by_graph(xg(u)), rows4(g2_rows, u), ALU.mult).then_inc(x_step, 1)

        def shift_x(eng, u):
            hold(eng, x_step, 2 * u + 2)
            eng.tensor_tensor(by_graph(xg(u)), by_graph(xg(u)), rows4(beta2_rows, u), ALU.add).then_inc(x_step, 1)

        ctx.enter_context(nc.allow_non_contiguous_dma(reason="3072 small parameters go down the partitions, once"))
        block = ctx.enter_context(nc.Block())

        def rows_of(src):
            return src.rearrange("(o l) d -> o l d", o=1).broadcast_to([P, L, src.shape[1]])

        @block.sync
        def _(sp):
            def load_x(g, count, landed):
                sp.dma_start(X[:, g * GD:(g + count) * GD].rearrange("p (b d) -> p b d", b=count * G),
                             x[g * G:(g + count) * G, :, :].rearrange("b i d -> i b d")).then_inc(landed, 16)

            def load_adj(u):
                need(sp, blocked_done, u)
                sp.dma_start(by_graph(adj_in[:, :]),
                             adj[bass.ds(group(u) * G, G), :, :].rearrange("b i j -> i b j")
                             ).then_inc(adj_landed, 16)

            def load_weights(l):
                need(sp, w1_split, l)
                sp.dma_start(w1_raw[:, :, :], W1[bass.ds(l, 1), :, :].rearrange("o (k p) f -> p (o k) f", p=P)
                             ).then_inc(w1_in, 16)
                need(sp, w2_split, l)
                sp.dma_start(w2_raw[:, :, :], W2[bass.ds(l, 1), :, :].rearrange("o (k p) d -> p (o k) d", p=P)
                             ).then_inc(w2_in, 16)

            def start():
                def attn_rows(first, last, landed):
                    for tile, src in ((wi_rows, attn_w[first:last, 0:D]), (wj_rows, attn_w[first:last, D:2 * D])):
                        sp.dma_start(tile[:, first:last, :], src.rearrange("(o l) d -> o l d", o=1)
                                     .broadcast_to([P, last - first, D])).then_inc(landed, 16)

                load_x(0, 1, x_in[0])
                attn_rows(0, 1, attn_in)
                sp.dma_start(bias_attn[:, :], attn_b.rearrange("(o l) -> o l", o=1).broadcast_to([P, L])
                             ).then_inc(attn_in, 16)
                load_adj(0)
                load_x(1, 1, x_in[1])
                sp.dma_start(by_graph(adj_second[:, :]), adj[G:2 * G, :, :].rearrange("b i j -> i b j")
                             ).then_inc(adj_second_in, 16)
                load_x(2, 2, x_in[2])
                sp.wait_ge(rows_in, 16 * N_ROWS)
                sp.wait_ge(w2_in, 16)
                sp.wait_ge(adj_landed, 16)
                load_adj(2)
                attn_rows(1, L, x_in[3])
                load_x(4, NG - 4, x_in[3])
                sp.wait_ge(adj_landed, 32)

            def step(t, dots=True, scores=True, mix=True, mlp=True, close=True, out=False, write=False,
                     next_w1=None, next_w2=None, update=True, before_last=False):
                if next_w1 is not None:
                    load_weights(next_w1)
                if out:
                    need(sp, res3_done, t - 2 - LAST)
                    sp.dma_start(by_graph(x_input),
                                 x[bass.ds(group(t - 2) * G, G), :, :].rearrange("b i d -> i b d")).then_inc(y_in, 16)
                if dots:
                    load_adj(t + 3)
                if before_last:
                    sp.wait_ge(res1_done, G * U)
                    sp.dma_start(by_graph(xg(U - 1)), x[B - G:B, :, :].rearrange("b i d -> i b d")
                                 ).then_inc(last_input_in, 16)
                if out:
                    hold(sp, y_in, 16 * (t - 2 - LAST) + 16)
                if write:
                    u = t - 3
                    sp.wait_ge(y_done, G * (u - LAST) + G)
                    sp.dma_start(y_dram[bass.ds(group(u) * G, G), :, :].rearrange("b i d -> i b d"), by_graph(y)
                                 ).then_inc(stored, 16)
                    hold(sp, stored, 16 * (u - LAST) + 16)
                if dots:
                    hold(sp, adj_landed, 16 * t + 48)

            def finish():
                for i in range(2):
                    graphs = slice(B - G + i * G // 2, B - G + (i + 1) * G // 2)
                    sp.wait_ge(last_y_done[i], G // 2)
                    sp.dma_start(y_dram[graphs, :, :].rearrange("b i d -> i b d"),
                                 by_graph(xg(U - 1))[:, i * G // 2:(i + 1) * G // 2, :]).then_inc(stored, 16)
                sp.wait_ge(stored, 16 * (NG + 1))

            run_steps(sp, start, step, finish)

        @block.gpsimd
        def _(pool):
            def offsets(u):
                pool.wait_ge(blocked_done, u + 1)
                hold(pool, neg_si_done, u + 1)
                for b in range(G):
                    pool.tensor_scalar(offset[:, b * N:(b + 1) * N], offset[:, b * N:(b + 1) * N], MASKED,
                                       neg_si[:, b:b + 1], ALU.mult, ALU.add).then_inc(offset_done, 1)

            def split(raw, hi, lo, n, hi_done, lo_done):
                pool.tensor_scalar(hi, raw, 1.0, 0.0, ALU.mult, ALU.add).then_inc(hi_done, 1)
                pool.wait_ge(hi_done, n + 1)
                pool.tensor_tensor(lo, raw, hi.bitcast(F32), ALU.subtract).then_inc(lo_done, 1)

            def split_w1(l):
                pool.wait_ge(w1_in, 16 * l + 16)
                hold(pool, hid_mm, l * (NG * KF))
                split(w1_raw[:, :, :], w1_hi[:, :, :], w1_lo[:, :, :], l, w1_hi_done, w1_split)

            def split_w2(l):
                pool.wait_ge(w2_in, 16 * l + 16)
                hold(pool, mlp_mm, l * (NG * 2))
                split(w2_raw[:, :, :], w2_hi[:, :, :], w2_lo[:, :, :], l, w2_hi_done, w2_split)

            def scales(n, first, moments_done, moments, scratch, norm_step, scratch_used):
                var, rstd, nmean, shift = (scratch[:, i, :] for i in range(4))
                pool.wait_ge(moments_done, G * n + G + first)
                hold(pool, scratch_used, G * n + first)
                pool.tensor_scalar(var, moments[:, :, 1], EPS, None, ALU.add).then_inc(norm_step, 1)
                pool.tensor_scalar(nmean, moments[:, :, 0], -1.0, None, ALU.mult).then_inc(norm_step, 1)
                pool.wait_ge(norm_step, 4 * n + 2 + first)
                pool.tensor_tensor(rstd, var, minus_half[:, :], ALU.pow).then_inc(norm_step, 1)
                pool.wait_ge(norm_step, 4 * n + 3 + first)
                pool.tensor_tensor(shift, nmean, rstd, ALU.mult).then_inc(norm_step, 1)

            def scales1(u):
                scales(u, 0, moments1_done, moments1, scratch1, norm1_step, z1_done)

            def scales2(u):
                pool.wait_ge(x_step, 2 * u + 1)
                scales(u, 1, moments2_done, moments2, scratch2, norm2_step, z2_done)

            def normalise3(u):
                n = u - LAST
                scales(n, 0, moments3_done, moments3, scratch3, norm3_step, y_done)
                hold(pool, norm3_step, 4 * n + 4)
                for b in range(G):
                    pool.tensor_scalar(y[:, b * D:(b + 1) * D], y[:, b * D:(b + 1) * D], scratch3[:, 1, b:b + 1],
                                       scratch3[:, 3, b:b + 1], ALU.mult, ALU.add).then_inc(y_done, 1)

            def shift_last_input():
                pool.wait_ge(last_input_in, 16)
                pool.tensor_tensor(by_graph(xg(U - 1)), by_graph(xg(U - 1)), rows4(beta2_rows, U - 1), ALU.add
                                   ).then_inc(last_input_done, 1)

            def normalise_last(i):
                for b in range(i * G // 2, (i + 1) * G // 2):
                    pool.tensor_scalar(xb(U - 1, b), xb(U - 1, b), scratch3[:, 1, b:b + 1], scratch3[:, 3, b:b + 1],
                                       ALU.mult, ALU.add).then_inc(last_y_done[i], 1)

            def scale_residual(u):
                pool.wait_ge(z1_done, G * u + G)
                hold(pool, res2_done, 2 * u)
                pool.tensor_tensor(by_graph(q[:, :]), by_graph(z1[:, :]), rows4(g1_rows, u), ALU.mult
                                   ).then_inc(q_step, 1)

            def shift_residual(u):
                pool.wait_ge(c1_done, 1)
                hold(pool, q_step, 2 * u + 1)
                pool.tensor_tensor(by_graph(q[:, :]), by_graph(q[:, :]), rows4(c1_rows, u), ALU.add
                                   ).then_inc(q_step, 1)

            def start():
                for tile in (ident, neg_ident):
                    pool.memset(tile[:, :], 0.0).then_inc(ident_done, 1)
                pool.memset(minus_half[:, :], -0.5).then_inc(norm_const, 1)
                for i, free in enumerate((z2_done, x_step)):
                    pool.memset(res2[:, i:i + 1], 0.0).then_inc(free, 1)
                pool.memset(scratch2[:, 0, 0:1], 0.0).then_inc(norm2_step, 1)
                pool.wait_ge(ident_done, 2)
                for tile, fill in ((ident, 1.0), (neg_ident, -1.0)):
                    pool.affine_select(out=tile[:, :], in_=tile[:, :], compare_op=ALU.not_equal, fill=fill, base=0,
                                       pattern=[[-1, P]], channel_multiplier=1).then_inc(ident_done, 1)
                pool.wait_ge(norm_const, 1)
                offsets(0)
                split_w1(0)
                offsets(1)
                scales1(0)
                pool.wait_ge(rows_in, 16 * N_ROWS)
                pool.tensor_tensor(c1_rows[:, :, :], c1_rows[:, :, :], b2_rows[:, :, :], ALU.add).then_inc(c1_done, 1)
                split_w2(0)

            def step(t, dots=True, scores=True, mix=True, mlp=True, close=True, out=False, write=False,
                     next_w1=None, next_w2=None, update=True, before_last=False):
                if next_w2 is not None:
                    split_w2(next_w2)
                if mlp:
                    scale_residual(t)
                if scores:
                    offsets(t + 2)
                if mix:
                    scales1(t + 1)
                if next_w2 is not None:
                    shift_x(pool, t - 2)
                if close:
                    scales2(t - 1)
                if next_w1 is not None:
                    split_w1(next_w1)
                if mlp:
                    shift_residual(t)
                if out:
                    normalise3(t - 2)
                if before_last:
                    shift_last_input()
                if close and update and not before_last:
                    scale_x(pool, t - 1)
                    if next_w1 is None:
                        shift_x(pool, t - 1)

            def finish():
                n = U - 1 - LAST
                scales(n, 0, moments3_done, moments3, scratch3, norm3_step, y_done)
                pool.wait_ge(norm3_step, 4 * n + 4)
                normalise_last(1)

            run_steps(pool, start, step, finish)

        @block.scalar
        def _(act):
            def x_high(u):
                need(act, mix_mm, 2 * u)
                need(act, x_lo_done, u)
                act.activation(x_hi[:, :], xg(u), ACT.Copy).then_inc(x_hi_done, 1)

            def softmax_numerators(u):
                act.wait_ge(neg_max_done, u + 1)
                need(act, pt_mm, u)
                need(act, row_inv_done, u)
                for b in range(G):
                    act.activation(prob[:, b * N:(b + 1) * N], neg_scores[:, b * N:(b + 1) * N], ACT.Exp,
                                   bias=neg_max[:, b:b + 1], scale=-1.0, accum_out=row_sum[:, b:b + 1]
                                   ).then_inc(prob_done, 1)

            def pt_high(u):
                act.wait_ge(pt_mm, u + 1)
                need(act, mix_mm, 2 * u)
                need(act, pt_done, u)
                act.activation(pt_hi[:, :], ps_scores[:, :], ACT.Copy).then_inc(pt_hi_done, 1)

            def normalise(dst, src, scratch, done):
                for b in range(G):
                    act.activation(dst(b), src(b), ACT.Identity, bias=scratch[:, 3, b:b + 1],
                                   scale=scratch[:, 1, b:b + 1]).then_inc(done, 1)

            def normalise1(u):
                act.wait_ge(norm1_step, 4 * u + 4)
                need(act, zt_mm, u)
                need(act, q_step, 2 * u - 1)
                normalise((lambda b: z1[:, b * D:(b + 1) * D]), (lambda b: res1[:, b * D:(b + 1) * D]), scratch1,
                          z1_done)

            def normalise2(u):
                act.wait_ge(norm2_step, 4 * u + 5)
                normalise((lambda b: xb(u, b)), (lambda b: res2[:, b * D:(b + 1) * D]), scratch2, z2_done)

            def h_high(u):
                act.wait_ge(zt_mm, u + 1)
                for k in range(KD):
                    act.activation(ps_mix[:, k, :], ps_mix[:, k, :], ACT.Identity, bias=col(beta1_cols, u, k),
                                   scale=col(g1_cols, u, k)).then_inc(ht_step, 1)
                need(act, hid_mm, KF * u)
                need(act, ht_lo_done, u)
                act.wait_ge(ht_step, KD * u + KD)
                act.activation(ht_hi[:, :, :], ps_mix[:, :, :], ACT.Copy).then_inc(ht_hi_done, 1)

            def gelu(u, c):
                act.wait_ge(hid_mm, KF * u + c + 1)
                if c == 0:
                    need(act, mlp_mm, 2 * u)
                act.activation(ps_hid[c % 3][:, :], ps_hid[c % 3][:, :], ACT.Gelu, bias=col(b1_cols, u, c)
                               ).then_inc(gelu_done, 1)
                act.wait_ge(gelu_done, KF * u + c + 1)
                act.activation(act_hi[:, c, :], ps_hid[c % 3][:, :], ACT.Copy).then_inc(act_hi_done, 1)

            def load_table(func):
                act.activation(table_junk[:, 0:1], ident[:, 0:1], func)

            def start():
                def param(dst, src):
                    act.dma_start(dst, src).then_inc(rows_in, 16)

                def column(dst, src):
                    act.dma_start(dst, src).then_inc(cols_in, 16)

                for k in range(KD):
                    column(g1_cols[:, :, k], g1[:, k * P:(k + 1) * P].rearrange("l p -> p l"))
                    column(beta1_cols[:, :, k], beta1[:, k * P:(k + 1) * P].rearrange("l p -> p l"))
                act.dma_start(w1_raw[:, :, :], W1[0, :, :].rearrange("(k p) f -> p k f", p=P)).then_inc(w1_in, 16)
                for l in range(L):
                    column(b1_cols[:, l, :], b1[l, :].rearrange("(k p) -> p k", p=P))
                act.wait_ge(ident_done, 4)
                load_table(ACT.Exp)
                for tile, src in ((g1_rows, g1), (c1_rows, beta1), (g2_rows, g2), (beta2_rows, beta2)):
                    param(tile[:, :, :], rows_of(src))
                param(b2_rows[:, :, :], rows_of(b2))
                act.dma_start(w2_raw[:, :, :], W2[0, :, :].rearrange("(k p) d -> p k d", p=P)).then_inc(w2_in, 16)
                act.wait_ge(x_in[0], 16)
                x_high(0)
                softmax_numerators(0)
                pt_high(0)
                act.wait_ge(x_in[1], 16)
                x_high(1)
                normalise1(0)
                softmax_numerators(1)
                act.wait_ge(cols_in, 16 * N_COLS)
                h_high(0)
                pt_high(1)
                load_table(ACT.Gelu)

            def step(t, dots=True, scores=True, mix=True, mlp=True, close=True, out=False, write=False,
                     next_w1=None, next_w2=None, update=True, before_last=False):
                if mlp:
                    for c in range(KF):
                        gelu(t, c)
                if scores:
                    x_high(t + 2)
                if mix:
                    normalise1(t + 1)
                if scores:
                    softmax_numerators(t + 2)
                if mix:
                    h_high(t + 1)
                if scores:
                    pt_high(t + 2)
                if close and update:
                    normalise2(t - 1)
                if mix:
                    load_table(ACT.Gelu)

            def finish():
                act.wait_ge(norm3_step, 4 * (U - 1 - LAST) + 4)
                for b in range(G // 2):
                    act.activation(xb(U - 1, b), xb(U - 1, b), ACT.Identity, bias=scratch3[:, 3, b:b + 1],
                                   scale=scratch3[:, 1, b:b + 1]).then_inc(last_y_done[0], 1)

            run_steps(act, start, step, finish)

        @block.vector
        def _(dve):
            def token_dots(u):
                first_units = isinstance(u, int) and u < 4
                dve.wait_ge(x_in[min(u, 2) if first_units else 3], 16 if first_units else 48)
                need(dve, neg_si_done, u)
                need(dve, scores_mm, u)
                for n in range(2 * G):
                    b = n % G
                    weights, dot = (wi_rows, si_raw) if n < G else (wj_rows, neg_sj)
                    need(dve, dots_done, 2 * G * u + n - 1)
                    dve.scalar_tensor_tensor(dot_junk[:, n % 2, :], xb(u, b), -1.0, row(weights, u), ALU.mult,
                                             ALU.mult, accum_out=dot[:, b:b + 1]).then_inc(dots_done, 1)
                dve.wait_ge(dots_done, 2 * G * u + G)
                need(dve, offset_done, G * u)
                dve.tensor_scalar(neg_si[:, :], si_raw[:, :], bias_attn[:, bass.ds(layer(u), 1)], None, ALU.subtract
                                  ).then_inc(neg_si_done, 1)

            def compare(u):
                second = isinstance(u, int) and u == 1
                if second:
                    dve.wait_ge(adj_second_in, 16)
                else:
                    dve.wait_ge(adj_landed, 16 if isinstance(u, int) and u == 0 else 16 * u)
                need(dve, neg_scores_done, u)
                dve.tensor_tensor(by_graph(offset[:, :]), by_graph(adj_second[:, :] if second else adj_in[:, :]),
                                  neg_ident[:, :].unsqueeze(1).broadcast_to([P, G, N]), ALU.is_le
                                  ).then_inc(blocked_done, 1)

            def masked_scores(u):
                dve.wait_ge(scores_mm, u + 1)
                dve.wait_ge(offset_done, G * u + G)
                need(dve, prob_done, G * u)
                dve.tensor_tensor(neg_scores[:, :], ps_scores[:, :], offset[:, :], ALU.add).then_inc(neg_scores_done, 1)

            def leaky_minimum(u):
                dve.wait_ge(neg_scores_done, u + 1)
                dve.scalar_tensor_tensor(neg_scores[:, :], neg_scores[:, :], SLOPE, neg_scores[:, :], ALU.mult, ALU.min
                                         ).then_inc(leaky_done, 1)
                dve.wait_ge(leaky_done, u + 1)
                dve.tensor_reduce(neg_max[:, :], by_graph(neg_scores[:, :]), AX_X, ALU.min).then_inc(neg_max_done, 1)

            def invert_sums(u):
                dve.wait_ge(prob_done, G * u + G)
                need(dve, res1_done, G * u)
                dve.reciprocal(row_inv[:, :], row_sum[:, :]).then_inc(row_inv_done, 1)

            def x_low(u):
                dve.wait_ge(x_hi_done, u + 1)
                need(dve, mix_mm, 2 * u)
                dve.tensor_tensor(x_lo[:, :], xg(u), x_hi[:, :].bitcast(F32), ALU.subtract).then_inc(x_lo_done, 1)

            def pt_low(u):
                dve.wait_ge(pt_hi_done, u + 1)
                need(dve, mix_mm, 2 * u)
                dve.tensor_tensor(pt_lo[:, :], ps_scores[:, :], pt_hi[:, :].bitcast(F32), ALU.subtract
                                  ).then_inc(pt_done, 1)

            def add_mix(u, i):
                if i == 0:
                    dve.wait_ge(row_inv_done, u + 1)
                    need(dve, z1_done, G * u)
                dve.wait_ge(mix_mm, 2 * u + i + 1)
                for b in range(i * G // 2, (i + 1) * G // 2):
                    dve.scalar_tensor_tensor(res1[:, b * D:(b + 1) * D], ps_mix[:, b // 2, (b % 2) * D:(b % 2 + 1) * D],
                                             row_inv[:, b:b + 1], xb(u, b), ALU.mult, ALU.add).then_inc(res1_done, 1)

            def statistics(n, first, src, src_done, per_src, stats, stats_done, moments_done):
                need(dve, moments_done, G * n + first)
                for b in range(G):
                    if b % (G // per_src) == 0:
                        (hold if per_src == 1 else need)(dve, src_done, per_src * n + b // (G // per_src) + 1)
                    dve.bn_stats(stats[:, b, :], src(b)).then_inc(stats_done, 1)

            def aggregate(n, first, stats, stats_done, moments, moments_done, norm_step):
                need(dve, norm_step, 4 * n + first)
                hold(dve, stats_done, G * n + G)
                for b in range(G):
                    dve.bn_aggr(moments[:, b, :], stats[:, b, :]).then_inc(moments_done, 1)

            def statistics1(u):
                statistics(u, 0, (lambda b: res1[:, b * D:(b + 1) * D]), res1_done, G, stats1, stats1_done,
                           moments1_done)

            def aggregate1(u):
                aggregate(u, 0, stats1, stats1_done, moments1, moments1_done, norm1_step)

            def h_low(u):
                dve.wait_ge(ht_hi_done, u + 1)
                need(dve, hid_mm, KF * u)
                dve.tensor_tensor(ht_lo[:, :, :], ps_mix[:, :, :], ht_hi[:, :, :].bitcast(F32), ALU.subtract
                                  ).then_inc(ht_lo_done, 1)

            def act_low(u, c):
                dve.wait_ge(act_hi_done, KF * u + c + 1)
                if c == 0:
                    need(dve, mlp_mm, 2 * u)
                dve.tensor_tensor(act_lo[:, c, :], ps_hid[c % 3][:, :], act_hi[:, c, :].bitcast(F32), ALU.subtract
                                  ).then_inc(act_lo_done, 1)

            def add_mlp(u):
                dve.wait_ge(q_step, 2 * u + 2)
                dve.wait_ge(z2_done, G * u + 1)
                for i in range(2):
                    dve.wait_ge(mlp_mm, 2 * u + i + 1)
                    dve.tensor_tensor(res2[:, i * T:(i + 1) * T], ps_mlp[:, i, :], q[:, i * T:(i + 1) * T], ALU.add
                                      ).then_inc(res2_done, 1)

            def statistics2(u):
                statistics(u, 1, (lambda b: res2[:, b * D:(b + 1) * D]), res2_done, 2, stats2, stats2_done,
                           moments2_done)

            def aggregate2(u):
                aggregate(u, 1, stats2, stats2_done, moments2, moments2_done, norm2_step)

            def add_last_input(u):
                dve.wait_ge(norm2_step, 4 * u + 5)
                for b in range(G):
                    dve.scalar_tensor_tensor(res2[:, b * D:(b + 1) * D], res2[:, b * D:(b + 1) * D],
                                             scratch2[:, 2, b:b + 1], row(g2_rows, u), ALU.add, ALU.mult
                                             ).then_inc(last_scaled, 1)
                dve.wait_ge(last_input_done, 1)
                for b in range(G):
                    dve.wait_ge(last_scaled, b + 1)
                    last = dve.scalar_tensor_tensor(xb(u, b), res2[:, b * D:(b + 1) * D], scratch2[:, 1, b:b + 1],
                                                    xb(u, b), ALU.mult, ALU.add)
                last.then_inc(res3_done, 1)

            def add_input(u):
                n = u - LAST
                dve.wait_ge(x_step, 2 * u + 3)
                dve.wait_ge(y_in, 16 * n + 16)
                need(dve, stored, 16 * n)
                dve.tensor_tensor(y, xg(u), x_input, ALU.add).then_inc(res3_done, 1)

            def statistics3(u, src=lambda b: y[:, b * D:(b + 1) * D]):
                n = u - LAST
                statistics(n, 0, src, res3_done, 1, stats3, stats3_done, moments3_done)

            def aggregate3(u):
                aggregate(u - LAST, 0, stats3, stats3_done, moments3, moments3_done, norm3_step)

            def start():
                dve.memset(moments2[:, :, :], 0.0).then_inc(moments2_done, 1)
                dve.wait_ge(ident_done, 4)
                dve.wait_ge(attn_in, 48)
                token_dots(0)
                compare(0)
                masked_scores(0)
                leaky_minimum(0)
                x_low(0)
                invert_sums(0)
                pt_low(0)
                token_dots(1)
                compare(1)
                add_mix(0, 0)
                add_mix(0, 1)
                statistics1(0)
                aggregate1(0)
                masked_scores(1)
                leaky_minimum(1)
                x_low(1)
                h_low(0)
                invert_sums(1)
                pt_low(1)
                token_dots(2)

            def step(t, dots=True, scores=True, mix=True, mlp=True, close=True, out=False, write=False,
                     next_w1=None, next_w2=None, update=True, before_last=False):
                def low(c):
                    if mlp:
                        act_low(t, c)

                if close:
                    add_mlp(t - 1)
                low(0)
                if close and mix:
                    statistics2(t - 1)
                low(1)
                if mix:
                    add_mix(t + 1, 0)
                low(2)
                if mix:
                    add_mix(t + 1, 1)
                low(3)
                if scores:
                    compare(t + 2)
                low(4)
                if mix:
                    statistics1(t + 1)
                elif close:
                    statistics2(t - 1)
                if close:
                    aggregate2(t - 1)
                if mix:
                    aggregate1(t + 1)
                for c in range(5, KF):
                    low(c)
                if scores:
                    masked_scores(t + 2)
                if out:
                    add_input(t - 2)
                elif scores:
                    x_low(t + 2)
                if scores:
                    leaky_minimum(t + 2)
                if out:
                    statistics3(t - 2)
                    if scores:
                        x_low(t + 2)
                    aggregate3(t - 2)
                if before_last:
                    scale_x(dve, t - 1)
                    shift_x(dve, t - 1)
                if scores:
                    invert_sums(t + 2)
                if dots:
                    token_dots(t + 3)
                if mix:
                    h_low(t + 1)
                if scores:
                    pt_low(t + 2)

            def finish():
                add_last_input(U - 1)
                statistics3(U - 1, lambda b: xb(U - 1, b))
                aggregate3(U - 1)

            run_steps(dve, start, step, finish)

        @block.tensor
        def _(pe):
            def split_product(dst, products, done=None):
                last = None
                for n, (stationary, moving) in enumerate(products):
                    last = pe.matmul(dst, stationary, moving, start=(n == 0), stop=(n == len(products) - 1))
                if done is not None:
                    last.then_inc(done, 1)

            def spread_scores(u):
                pe.wait_ge(dots_done, 2 * G * u + 2 * G)
                need(pe, pt_done, u)
                for b in range(G):
                    last = pe.transpose(ps_scores[:, b * N:(b + 1) * N], neg_sj[:, b:b + 1].broadcast_to([P, N]),
                                        ident[:, :])
                last.then_inc(scores_mm, 1)

            def transpose_probs(u):
                pe.wait_ge(prob_done, G * u + G)
                pe.wait_ge(neg_scores_done, u + 1)
                for b in range(G):
                    last = pe.transpose(ps_scores[:, b * N:(b + 1) * N], prob[:, b * N:(b + 1) * N], ident[:, :])
                last.then_inc(pt_mm, 1)

            def mix_neighbours(u):
                pe.wait_ge(pt_done, u + 1)
                pe.wait_ge(x_lo_done, u + 1)
                need(pe, ht_lo_done, u)
                for b in range(G):
                    tok, feat = slice(b * N, (b + 1) * N), slice(b * D, (b + 1) * D)
                    split_product(ps_mix[:, b // 2, (b % 2) * D:(b % 2 + 1) * D],
                                  [(pt_hi[:, tok], x_hi[:, feat]), (pt_hi[:, tok], x_lo[:, feat]),
                                   (pt_lo[:, tok], x_hi[:, feat])],
                                  mix_mm if b % 2 else None)

            def transpose_z(u):
                pe.wait_ge(z1_done, G * u + G)
                pe.wait_ge(res1_done, G * u + G)
                for k in range(KD):
                    for b in range(G):
                        last = pe.transpose(ps_mix[:, k, b * N:(b + 1) * N], z1[:, b * D + k * P:b * D + (k + 1) * P],
                                            ident[:, :])
                last.then_inc(zt_mm, 1)

            def first_product(u, c):
                cols = slice(c * P, (c + 1) * P)
                dst = ps_hid[c % 3][:, :]
                if c == 0:
                    pe.wait_ge(w1_split, layer(u) + 1)
                    pe.wait_ge(ht_hi_done, u + 1)
                need(pe, act_lo_done, KF * u + max(c - 2, 0))
                for n, w in enumerate((w1_hi, w1_lo)):
                    for k in range(KD):
                        pe.matmul(dst, w[:, k, cols], ht_hi[:, k, :], start=(n + k == 0), stop=False)
                if c == 0:
                    pe.wait_ge(ht_lo_done, u + 1)
                for k in range(KD):
                    last = pe.matmul(dst, w1_hi[:, k, cols], ht_lo[:, k, :], start=False, stop=(k == KD - 1))
                last.then_inc(hid_mm, 1)

            def second_product(u, b):
                tok = slice(b * N, (b + 1) * N)
                dst = ps_mlp[:, b // 2, (b % 2) * D:(b % 2 + 1) * D]
                if b == 0:
                    pe.wait_ge(w2_split, layer(u) + 1)
                    need(pe, res2_done, 2 * u)
                for c in range(KF):
                    if b == 0:
                        pe.wait_ge(act_hi_done, KF * u + c + 1)
                    pe.matmul(dst, act_hi[:, c, tok], w2_hi[:, c, :], start=(c == 0), stop=False)
                    pe.matmul(dst, act_hi[:, c, tok], w2_lo[:, c, :], start=False, stop=False)
                for c in range(KF):
                    if b == 0:
                        pe.wait_ge(act_lo_done, KF * u + c + 1)
                    last = pe.matmul(dst, act_lo[:, c, tok], w2_hi[:, c, :], start=False, stop=(c == KF - 1))
                if b % 2:
                    last.then_inc(mlp_mm, 1)

            def start():
                pe.wait_ge(ident_done, 4)
                spread_scores(0)
                transpose_probs(0)
                mix_neighbours(0)
                spread_scores(1)
                transpose_z(0)
                transpose_probs(1)

            def step(t, dots=True, scores=True, mix=True, mlp=True, close=True, out=False, write=False,
                     next_w1=None, next_w2=None, update=True, before_last=False):
                if mlp:
                    first_product(t, 0)
                    first_product(t, 1)
                if mix:
                    mix_neighbours(t + 1)
                if mlp:
                    for c in range(2, KF):
                        first_product(t, c)
                if scores:
                    spread_scores(t + 2)
                if mlp:
                    second_product(t, 0)
                    second_product(t, 1)
                if mix:
                    transpose_z(t + 1)
                if mlp:
                    second_product(t, 2)
                if scores:
                    transpose_probs(t + 2)
                if mlp:
                    second_product(t, 3)

            def finish():
                pass

            run_steps(pe, start, step, finish)


_INS = ['x', 'adj', 'L0_gnn_attn_w', 'L0_gnn_attn_b', 'L0_gnn_W1', 'L0_gnn_b1', 'L0_gnn_W2', 'L0_gnn_b2',
        'L0_gnn_g1', 'L0_gnn_beta1', 'L0_gnn_g2', 'L0_gnn_beta2']
_OUTS = [((64, 128, 256), 'float32')]


def kernel(**inputs):
    import numpy as _np
    import concourse.bacc as _bacc
    from concourse import mybir as _mybir
    from concourse.bass_utils import run_bass_kernel_spmd as _run

    nc = _bacc.Bacc("TRN2", target_bir_lowering=False, num_devices=1, dynamic_dma_scratch_size=1024)
    arrays, args = {}, []
    for name in _INS:
        a = _np.ascontiguousarray(inputs[name])
        arrays[f"in_{name}_dram"] = a
        args.append(nc.dram_tensor(f"in_{name}_dram", a.shape, _mybir.dt.from_np(a.dtype), kind="ExternalInput").ap())
    for i, (shape, dtype) in enumerate(_OUTS):
        dt = _mybir.dt.from_np(_np.dtype(dtype))
        args.append(nc.dram_tensor(f"out_{i}_dram", shape, dt, kind="ExternalOutput").ap())
    gnn_layers_resnorm_kernel(nc, *args)
    r = _run(nc, [arrays], core_ids=[0])
    got = tuple(r.results[0][f"out_{i}_dram"] for i in range(len(_OUTS)))
    return got[0]
```
